# Optimizing a Trainium2 kernel written in Bass

```python
import numpy as np
import jax
import jax.numpy as jnp

def _softmax(x, axis=-1):
    return jax.nn.softmax(x, axis=axis)

def _gelu(x):
    return jax.nn.gelu(x, approximate=True)

def _silu(x):
    return jax.nn.silu(x)

def _sigmoid(x):
    return jax.nn.sigmoid(x)

def _layernorm(x, axis=-1, eps=1e-05):
    m = jnp.mean(x, axis=axis, keepdims=True)
    v = jnp.var(x, axis=axis, keepdims=True)
    return (x - m) / jnp.sqrt(v + eps)

def _scatter_add(tgt, idx, src, axis=0):
    return tgt.at[idx].add(src)

def _segment_sum(src, seg, n):
    return jax.ops.segment_sum(src, seg, n)
kernel_name = 'mk_xattn_seq_d2_seqx_r2_edba4e'

def setup_inputs(seed: int=0):
    np.random.seed(seed)
    _w = jnp.asarray

    def _rec_inputs():
        import jax
        import jax.numpy as jnp
        _rk = jax.random.key(seed)
        x = -0.000125 + 0.9999 * jax.random.normal(jax.random.fold_in(_rk, 1), (2, 2048, 512), jnp.float32)
        _lenS = 2048 - jax.random.randint(jax.random.fold_in(_rk, 7), (2,), 0, max(1, 2048 // 4) + 1, jnp.int32)
        _lenS2 = 128 - jax.random.randint(jax.random.fold_in(_rk, 8), (2,), 0, max(1, 128 // 4) + 1, jnp.int32)
        _ctx_2048P = jax.random.normal(jax.random.fold_in(_rk, 11), (2, 16, 1024), jnp.float32)
        _ctx_2048c = jax.random.dirichlet(jax.random.fold_in(_rk, 511), 0.3 * jnp.ones((16,), jnp.float32), (2, 128))
        _ctx_2048t = jnp.einsum('bsk,bkd->bsd', _ctx_2048c, _ctx_2048P)
        _ctx_2048t = _ctx_2048t * jax.lax.rsqrt(jnp.mean(jnp.square(_ctx_2048t)) + 1e-12) * 0.953939
        ctx_2048 = 5.36139e-06 + 1.00015 * (_ctx_2048t + 0.3 * jax.random.normal(jax.random.fold_in(_rk, 611), (2, 128, 1024), jnp.float32))
        _validS = jnp.arange(2048)[None, :] < _lenS[:, None]
        _validS2 = jnp.arange(128)[None, :] < _lenS2[:, None]
        _causal = jnp.tril(jnp.ones((2048, 2048), dtype=bool))
        mask_S_fk1 = jnp.where(_validS[0], 1.0, 0.0).astype(jnp.float32)
        mask_S_fk0 = jnp.where(_validS[0], 0.0, 1.0).astype(jnp.float32)
        return (x, ctx_2048, mask_S_fk1, mask_S_fk0)
    x, ctx_2048, mask_S_fk1, mask_S_fk0 = _rec_inputs()

    def _L0_xattn_setup():
        import jax, jax.numpy as jnp
        import numpy as np
        HEADS = 16
        HEAD_DIM = 64
        SUPPRESS = 20.0
        key = jax.random.key(seed)
        ks = jax.random.split(key, 8)
        B, HW, C, T, CT = (8, 2048, 512, 77, 1024)
        inner = HEADS * HEAD_DIM
        scale = 0.02
        return {'hidden_states': jax.random.normal(ks[0], (B, HW, C), jnp.float32), 'encoder_hidden_states': jax.random.normal(ks[1], (B, T, CT), jnp.float32), 'mask_A': (jax.random.uniform(ks[2], (HW,)) > 0.5).astype(jnp.float32), 'mask_B': (jax.random.uniform(ks[3], (HW,)) > 0.5).astype(jnp.float32), 'Wq': jax.random.normal(ks[4], (C, inner), jnp.float32) * scale, 'Wk': jax.random.normal(ks[5], (CT, inner), jnp.float32) * scale, 'Wv': jax.random.normal(ks[6], (CT, inner), jnp.float32) * scale, 'Wo': jax.random.normal(ks[7], (inner, C), jnp.float32) * scale, 'bo': jnp.zeros((C,), jnp.float32), 'token_indices_A': jnp.array([2, 3], dtype=jnp.int64), 'token_indices_B': jnp.array([5, 6], dtype=jnp.int64)}
    _L0_xattn_all = _L0_xattn_setup()
    _L0_xattn_in = {k: v for k, v in _L0_xattn_all.items() if k in ('Wq', 'Wk', 'Wv', 'Wo', 'bo', 'token_indices_A', 'token_indices_B')}
    del _L0_xattn_all

    def _L1_xattn_setup():
        import jax, jax.numpy as jnp
        import numpy as np
        HEADS = 16
        HEAD_DIM = 64
        SUPPRESS = 20.0
        key = jax.random.key(seed)
        ks = jax.random.split(key, 8)
        B, HW, C, T, CT = (8, 2048, 512, 77, 1024)
        inner = HEADS * HEAD_DIM
        scale = 0.02
        return {'hidden_states': jax.random.normal(ks[0], (B, HW, C), jnp.float32), 'encoder_hidden_states': jax.random.normal(ks[1], (B, T, CT), jnp.float32), 'mask_A': (jax.random.uniform(ks[2], (HW,)) > 0.5).astype(jnp.float32), 'mask_B': (jax.random.uniform(ks[3], (HW,)) > 0.5).astype(jnp.float32), 'Wq': jax.random.normal(ks[4], (C, inner), jnp.float32) * scale, 'Wk': jax.random.normal(ks[5], (CT, inner), jnp.float32) * scale, 'Wv': jax.random.normal(ks[6], (CT, inner), jnp.float32) * scale, 'Wo': jax.random.normal(ks[7], (inner, C), jnp.float32) * scale, 'bo': jnp.zeros((C,), jnp.float32), 'token_indices_A': jnp.array([2, 3], dtype=jnp.int64), 'token_indices_B': jnp.array([5, 6], dtype=jnp.int64)}
    _L1_xattn_all = _L1_xattn_setup()
    _L1_xattn_in = {k: v for k, v in _L1_xattn_all.items() if k in ('Wq', 'Wk', 'Wv', 'Wo', 'bo', 'token_indices_A', 'token_indices_B')}
    del _L1_xattn_all
    return {'x': x, 'ctx_2048': ctx_2048, 'mask_S_fk1': mask_S_fk1, 'mask_S_fk0': mask_S_fk0, 'L0_xattn_Wq': _L0_xattn_in['Wq'], 'L0_xattn_Wk': _L0_xattn_in['Wk'], 'L0_xattn_Wv': _L0_xattn_in['Wv'], 'L0_xattn_Wo': _L0_xattn_in['Wo'], 'L0_xattn_bo': _L0_xattn_in['bo'], 'L0_xattn_token_indices_A': _L0_xattn_in['token_indices_A'], 'L0_xattn_token_indices_B': _L0_xattn_in['token_indices_B'], 'L1_xattn_Wq': _L1_xattn_in['Wq'], 'L1_xattn_Wk': _L1_xattn_in['Wk'], 'L1_xattn_Wv': _L1_xattn_in['Wv'], 'L1_xattn_Wo': _L1_xattn_in['Wo'], 'L1_xattn_bo': _L1_xattn_in['bo'], 'L1_xattn_token_indices_A': _L1_xattn_in['token_indices_A'], 'L1_xattn_token_indices_B': _L1_xattn_in['token_indices_B']}

def reference(x, ctx_2048, mask_S_fk1, mask_S_fk0, L0_xattn_Wq, L0_xattn_Wk, L0_xattn_Wv, L0_xattn_Wo, L0_xattn_bo, L0_xattn_token_indices_A, L0_xattn_token_indices_B, L1_xattn_Wq, L1_xattn_Wk, L1_xattn_Wv, L1_xattn_Wo, L1_xattn_bo, L1_xattn_token_indices_A, L1_xattn_token_indices_B):
    import jax
    import jax.numpy as jnp

    def _L0_xattn_ref(hidden_states, encoder_hidden_states, mask_A, mask_B, Wq, Wk, Wv, Wo, bo, token_indices_A, token_indices_B):
        import jax, jax.numpy as jnp
        import numpy as np
        HEADS = 16
        HEAD_DIM = 64
        SUPPRESS = 20.0
        B, HW, C = hidden_states.shape
        T = encoder_hidden_states.shape[1]
        residual = hidden_states
        q = hidden_states @ Wq
        k = encoder_hidden_states @ Wk
        v = encoder_hidden_states @ Wv
        q = q.reshape(B, HW, HEADS, HEAD_DIM).transpose(0, 2, 1, 3)
        k = k.reshape(B, T, HEADS, HEAD_DIM).transpose(0, 2, 1, 3)
        v = v.reshape(B, T, HEADS, HEAD_DIM).transpose(0, 2, 1, 3)
        scale = HEAD_DIM ** (-0.5)
        logits = jnp.einsum('bhqd,bhkd->bhqk', q, k) * scale
        suppress_A_in = 1.0 - mask_A
        suppress_B_in = 1.0 - mask_B
        col_bias = jnp.zeros((HW, T), logits.dtype)
        col_bias = col_bias.at[:, token_indices_A].set((-SUPPRESS * suppress_A_in)[:, None])
        col_bias = col_bias.at[:, token_indices_B].set((-SUPPRESS * suppress_B_in)[:, None])
        logits = logits + col_bias[None, None, :, :]
        probs = jax.nn.softmax(logits, axis=-1)
        out = jnp.einsum('bhqk,bhkd->bhqd', probs, v)
        out = out.transpose(0, 2, 1, 3).reshape(B, HW, HEADS * HEAD_DIM)
        out = out @ Wo + bo
        out = out + residual
        return out

    def _L1_xattn_ref(hidden_states, encoder_hidden_states, mask_A, mask_B, Wq, Wk, Wv, Wo, bo, token_indices_A, token_indices_B):
        import jax, jax.numpy as jnp
        import numpy as np
        HEADS = 16
        HEAD_DIM = 64
        SUPPRESS = 20.0
        B, HW, C = hidden_states.shape
        T = encoder_hidden_states.shape[1]
        residual = hidden_states
        q = hidden_states @ Wq
        k = encoder_hidden_states @ Wk
        v = encoder_hidden_states @ Wv
        q = q.reshape(B, HW, HEADS, HEAD_DIM).transpose(0, 2, 1, 3)
        k = k.reshape(B, T, HEADS, HEAD_DIM).transpose(0, 2, 1, 3)
        v = v.reshape(B, T, HEADS, HEAD_DIM).transpose(0, 2, 1, 3)
        scale = HEAD_DIM ** (-0.5)
        logits = jnp.einsum('bhqd,bhkd->bhqk', q, k) * scale
        suppress_A_in = 1.0 - mask_A
        suppress_B_in = 1.0 - mask_B
        col_bias = jnp.zeros((HW, T), logits.dtype)
        col_bias = col_bias.at[:, token_indices_A].set((-SUPPRESS * suppress_A_in)[:, None])
        col_bias = col_bias.at[:, token_indices_B].set((-SUPPRESS * suppress_B_in)[:, None])
        logits = logits + col_bias[None, None, :, :]
        probs = jax.nn.softmax(logits, axis=-1)
        out = jnp.einsum('bhqk,bhkd->bhqd', probs, v)
        out = out.transpose(0, 2, 1, 3).reshape(B, HW, HEADS * HEAD_DIM)
        out = out @ Wo + bo
        out = out + residual
        return out
    x = _L0_xattn_ref(x, ctx_2048, mask_S_fk1, mask_S_fk0, L0_xattn_Wq, L0_xattn_Wk, L0_xattn_Wv, L0_xattn_Wo, L0_xattn_bo, L0_xattn_token_indices_A, L0_xattn_token_indices_B)
    x = _L1_xattn_ref(x, ctx_2048, mask_S_fk1, mask_S_fk0, L1_xattn_Wq, L1_xattn_Wk, L1_xattn_Wv, L1_xattn_Wo, L1_xattn_bo, L1_xattn_token_indices_A, L1_xattn_token_indices_B)
    return x

_drawn_inputs = setup_inputs


def setup_inputs(seed=0):
    import zlib

    import numpy as np

    out = dict(_drawn_inputs(seed))
    spreads = {'L0_xattn_bo': (0.0, 0.1), 'L1_xattn_bo': (0.0, 0.1)}
    factors = {'mask_S_fk1': 8.0,
     'mask_S_fk0': 8.0,
     'L0_xattn_Wq': 2.787,
     'L0_xattn_Wk': 2.774,
     'L1_xattn_Wq': 2.725,
     'L1_xattn_Wk': 2.721}
    for name, (base, spread) in spreads.items():
        noise = np.random.default_rng([zlib.crc32(name.encode()), seed]).standard_normal(out[name].shape)
        drawn = base * np.exp(spread * noise) if base else spread * noise
        out[name] = jnp.asarray(drawn.astype(out[name].dtype))
    for name, factor in factors.items():
        out[name] = (out[name] * factor).astype(out[name].dtype)
    return out
```

```python
from contextlib import ExitStack

import concourse.bass as bass
from concourse import mybir

F32 = mybir.dt.float32
F32R = mybir.dt.float32r
I32 = mybir.dt.int32
ALU = mybir.AluOpType
ACT = mybir.ActivationFunctionType
AX_X = mybir.AxisListType.X

P = 128
LAYERS = 2
SUPPRESS = 20.0


def two_cross_attentions(nc, xT, ctxT, masks, Wk, Wv, Wq, Wo, bo, idx, yT):
    C, ROWS = xT.shape
    CT, BT = ctxT.shape
    HW = masks.shape[1]
    INNER = Wk.shape[2]
    B = ROWS // HW
    T = BT // B
    NI = idx.shape[1] // (2 * LAYERS)
    D = 64
    H = INNER // D
    PAIRS = H // 2
    Q = 512
    NCH = ROWS // Q
    CPB = HW // Q
    TOTAL = LAYERS * NCH
    XT = C // P
    KTL = CT // P
    NB = Q // P
    SCALE = float(D) ** -0.5
    SUP = 64
    MRW = 96
    AHEAD = 2
    NORM = 5
    assert T == P and PAIRS == 8 and XT == 4 and NB == 4 and NCH == 8 and B == 2

    km_d = nc.dram_tensor("km_d", (LAYERS * B, P, H * T), F32, kind="Internal").ap()
    kt_d = nc.dram_tensor("kt_d", (LAYERS * B, P, H * T), F32, kind="Internal").ap()
    v_d = nc.dram_tensor("v_d", (LAYERS * B, T, INNER), F32, kind="Internal").ap()
    sup_d = nc.dram_tensor("sup_d", (4, HW), F32, kind="Internal").ap()
    x1_d = nc.dram_tensor("x1_d", (C, ROWS), F32, kind="Internal").ap()

    with ExitStack() as ctx:
        def sb(name, shape, dt):
            return ctx.enter_context(nc.sbuf_tensor(name, shape, dt))

        def sem(name):
            return ctx.enter_context(nc.semaphore(name))

        wq_hi = sb("wq_hi", [P, PAIRS, XT, P], F32R)
        wq_lo = sb("wq_lo", [P, PAIRS, XT, P], F32R)
        wo_hi = sb("wo_hi", [P, 2, XT, 4, P], F32R)
        wo_lo = sb("wo_lo", [P, 2, XT, 4, P], F32R)
        km = sb("km", [P, H, T], F32R)
        kt = sb("kt", [P, H, T], F32R)
        v = sb("v", [P, INNER], F32)
        x_f = sb("x_f", [P, XT, Q], F32)
        x_hi = sb("x_hi", [P, XT, Q], F32R)
        x_lo = sb("x_lo", [P, XT, Q], F32R)
        qe = sb("qe", [P, 2, 2, Q], F32R)
        qt = sb("qt", [P, 2, 2, Q], F32R)
        probs = sb("probs", [P, 4, 2, Q], F32)
        o_f = sb("o_f", [P, 4, Q], F32)
        o_hi = sb("o_hi", [P, 8, Q], F32R)
        o_lo = sb("o_lo", [P, 8, Q], F32R)
        res = sb("res", [P, XT, Q], F32)
        w_st = sb("w_st", [P, 2, 4, P], F32)
        rec = sb("rec", [P, Q], F32)
        rec_hi = sb("rec_hi", [P, Q], F32R)
        rec_lo = sb("rec_lo", [P, Q], F32R)
        sup_c = sb("sup_c", [P, Q], F32R)
        mneg = sb("mneg", [P, 2, NB, 32], F32)
        ident = sb("ident", [P, P], F32)
        rsel = sb("rsel", [P, 4, P], F32R)
        ssel = sb("ssel", [P, 2, 32], F32)
        bo_s = sb("bo_s", [P, LAYERS, XT], F32)

        c_f = x_f[:, :, :].rearrange("p a (b n) -> p (a b) n", n=BT)
        c_hi = x_hi[:, :, :].rearrange("p a (b n) -> p (a b) n", n=BT)
        c_lo = x_lo[:, :, :].rearrange("p a (b n) -> p (a b) n", n=BT)
        stage = [res[:, 0:2, :], res[:, 2:4, :], o_f[:, 0:2, :], o_f[:, 2:4, :]]
        stage = [s.rearrange("p a b -> p (a b)") for s in stage]
        s_hi = [o_hi[:, 2 * i:2 * i + 2, :].rearrange("p a b -> p (a b)") for i in range(4)]
        s_lo = [o_lo[:, 2 * i:2 * i + 2, :].rearrange("p a b -> p (a b)") for i in range(4)]
        k_hi = qt[:, :, :, :].rearrange("p a b n -> p (a b n)")
        k_lo = qe[:, :, :, :].rearrange("p a b n -> p (a b n)")
        v_s = probs[:, 0:2, :, :].rearrange("p b n c -> p b (n c)")
        tok = rec
        ind = probs[:, 2, :, :].rearrange("p a n -> p (a n)")
        ind_a, ind_b, ind_n = (ind[:, i * T:(i + 1) * T] for i in range(3))
        idx_f = ind[:, 3 * T:3 * T + 2 * LAYERS * NI]
        idx_w = ind[:, 3 * T + 32:3 * T + 32 + 2 * LAYERS * NI]
        row_s = ind[:, 3 * T + 64:3 * T + 128]
        ints = probs[:, 3, 0, :].bitcast(I32)
        ext = sup_c[:, :].rearrange("p (l a t) -> p l a t", l=LAYERS, a=2)
        MR = 2 * HW // P
        m_f, m_hi, m_lo = w_st[0:MR, 0, 0, :], rec_hi[0:MR, 0:P], rec_lo[0:MR, 0:P]

        banks = [ctx.enter_context(nc.psum_tensor(f"bank{i}", [P, 512], F32)) for i in range(8)]
        q_ps, bc_ps, out_ps = banks[0], banks[2], banks[3]
        lg_ps = [banks[4], banks[5]]
        mx_ps = [banks[1], lg_ps[1]]
        pv_ps, sum_ps = banks[6], banks[7]

        c_in = sem("c_in")
        c_split = sem("c_split")
        w_in = [sem(f"w_in{i}") for i in range(4)]
        w_hi_done = sem("w_hi_done")
        w_lo_done = sem("w_lo_done")
        w_used = sem("w_used")
        k_hi_done = sem("k_hi_done")
        k_lo_done = sem("k_lo_done")
        k_out = sem("k_out")
        v_done = sem("v_done")
        v_out = sem("v_out")
        consts = sem("consts")
        pool_c = sem("pool_c")
        small_in = sem("small_in")
        sup_out = sem("sup_out")
        ext_out = sem("ext_out")
        x_in = sem("x_in")
        x_hi_done = sem("x_hi_done")
        x_lo_done = sem("x_lo_done")
        sup_in = sem("sup_in")
        km_in = [sem(f"km_in{i}") for i in range(2)]
        kt_in = [sem(f"kt_in{i}") for i in range(2)]
        v_in = [sem(f"v_in{i}") for i in range(2)]
        q_done = sem("q_done")
        qhi_done = sem("qhi_done")
        qlo_done = sem("qlo_done")
        qdup_done = sem("qdup_done")
        mz_done = sem("mz_done")
        mx_done = sem("mx_done")
        mred_done = sem("mred_done")
        mt_done = sem("mt_done")
        mrow_done = sem("mrow_done")
        lg_done = sem("lg_done")
        p_done = sem("p_done")
        pv_done = sem("pv_done")
        sum_done = sem("sum_done")
        oun_done = sem("oun_done")
        rec_raw = sem("rec_raw")
        rec_h = sem("rec_h")
        rec_done = sem("rec_done")
        bc_done = sem("bc_done")
        on_done = sem("on_done")
        oh_done = sem("oh_done")
        o_done = sem("o_done")
        out_done = sem("out_done")
        res_done = sem("res_done")
        r_in = [sem(f"r_in{i}") for i in range(XT)]
        y_out = [sem(f"y_out{i}") for i in range(XT)]
        sl_in = [[sem(f"{w}_sl_in{i}") for i in range(2)] for w in ("wq", "wo")]
        sl_hi = [sem("wq_sl_hi"), sem("wo_sl_hi")]
        sl_lo = [sem("wq_sl_lo"), sem("wo_sl_lo")]

        block = ctx.enter_context(nc.Block())

        W_TILES = 2 * KTL
        KV = LAYERS * W_TILES
        K_STORES = 3 * 2 * B
        EXTRA = 8
        BIAS_STEPS = 4
        DVE_CONSTS = BIAS_STEPS + 5 + 8 + 24 + LAYERS * (2 * (1 + 2 * NI) + 2 + 4)
        POOL_CONSTS = 10

        def need(eng, s, count):
            if not isinstance(count, int) or count > 0:
                eng.wait_ge(s, count)

        def pair(g, s, off):
            i = s + off
            dg, i = i // PAIRS, i % PAIRS
            c = g + dg
            if isinstance(c, int) and not 0 <= c < TOTAL:
                return None
            return c * PAIRS + i, c, i

        def chunks(eng, step):
            for s in (6, 7):
                step(-1, s, 0)
            for layer in range(LAYERS):
                g0 = layer * NCH
                alone = range(2) if layer == 0 else range(g0, g0 + 1)
                for g in alone:
                    for s in range(PAIRS):
                        step(g, s, layer)
                with eng.Fori(alone[-1] + 1, g0 + NCH - 1) as g:
                    for s in range(PAIRS):
                        step(g, s, layer)
                for s in range(PAIRS):
                    step(g0 + NCH - 1, s, layer)
            for s in range(PAIRS):
                step(TOTAL, s, LAYERS - 1)

        def layer_of(g, layer):
            return g // NCH if isinstance(g, int) else layer

        @block.sync
        def _(sp):
            sp.dma_start(c_f, ctxT.rearrange("(k p) n -> p k n", p=P)).then_inc(c_in, 16)

            def w_load(w, l):
                need(sp, w_lo_done, l * W_TILES + w - 3)
                kk = w % KTL
                src = (Wk if w < KTL else Wv)[l, kk * P:(kk + 1) * P, :]
                sp.dma_start(stage[w % 4], src).then_inc(w_in[w % 4], 16)

            def layer_loads(l, first):
                for w in range(W_TILES):
                    w_load(w, l)
                    if w == 1 and first:
                        sp.dma_start(m_f, masks.rearrange("a (r n) -> (a r) n", n=P)).then_inc(small_in, 16)
                        sp.dma_start(ints[:, 0:2 * LAYERS * NI],
                                     idx.partition_broadcast(P)).then_inc(small_in, 16)
                        sp.dma_start(bo_s[:, :, :], bo.rearrange("p (l t) -> p l t", t=XT)).then_inc(small_in, 16)
                    if w == W_TILES - 4:
                        need(sp, k_hi_done, 4 * (l + 1))
                        need(sp, k_lo_done, 4 * (l + 1))
                        for part, dst, row in ((k_hi, km_d, 0), (k_lo, kt_d, 0), (k_hi, kt_d, D)):
                            src = part.bitcast(F32).rearrange("p (m b t) -> p m b t", m=PAIRS, b=B)
                            for b in range(B):
                                rows = dst[l * B + b, row:row + D, :].rearrange("d (m h t) -> d m h t", h=2, t=T)
                                for h in range(2):
                                    sp.dma_start(rows[:, :, h, :], src[h * D:(h + 1) * D, :, b, :]).then_inc(k_out, 16)

            layer_loads(0, True)
            layer_loads(1, False)
            for j in range(8):
                need(sp, w_lo_done, KV + j - 3)
                if j < 4:
                    src, dst = Wq[0, j * P:(j + 1) * P, :], stage[j % 4]
                else:
                    src = Wo[0, (j - 4) * 2 * P:(j - 3) * 2 * P, :].rearrange("(a p) n -> p a n", p=P)
                    dst = stage[j % 4].rearrange("p (a n) -> p a n", a=2)
                sp.dma_start(dst, src).then_inc(w_in[j % 4], 16)
            sp.wait_ge(consts, BIAS_STEPS)
            for i, part in enumerate((m_hi, m_lo)):
                for a in range(2):
                    sp.dma_start(sup_d[2 * a + i, :].rearrange("(r n) -> r n", n=P),
                                 part[a * MR // 2:(a + 1) * MR // 2, :].bitcast(F32)).then_inc(sup_out, 16)

            def index(value):
                return value if isinstance(value, int) else sp.snap(value)

            def load_x(c, layer):
                need(sp, x_lo_done, XT * c)
                src = xT if layer == 0 else x1_d
                if layer:
                    for t in range(XT):
                        sp.wait_ge(y_out[t], 16 * (c - NCH + 1))
                col = (c - layer * NCH) * Q
                sp.dma_start(x_f[:, :, :], src[:, bass.ds(col, Q)].rearrange("(t p) n -> p t n", p=P)).then_inc(x_in, 16)

            def load_sup(c):
                at = index(c % CPB)
                need(sp, mz_done, 2 * PAIRS * c)
                sp.dma_start(sup_c[SUP:SUP + 4, :].bitcast(F32), sup_d[:, bass.ds(at * Q, Q)]).then_inc(sup_in, 16)

            def load_k(c, half):
                lb = index(c // CPB)
                need(sp, lg_done, 2 * (PAIRS * (c - 1) + 4 * (half + 1)))
                hs = slice(half * 8 * T, (half + 1) * 8 * T)
                dst = km[:, half * 8:half * 8 + 8, :].rearrange("p h t -> p (h t)").bitcast(F32)
                if isinstance(c, int) and c == 0:
                    sp.dma_start(dst[SUP:P, :], km_d[lb, SUP:P, hs]).then_inc(km_in[half], 16)
                else:
                    sp.dma_start(dst[SUP:SUP + 4, :], km_d[lb, SUP:SUP + 4, hs]).then_inc(km_in[half], 16)
                sp.dma_start(dst[0:D, :], km_d[lb, 0:D, hs]).then_inc(km_in[half], 16)
                sp.dma_start(kt[:, half * 8:half * 8 + 8, :].rearrange("p h t -> p (h t)").bitcast(F32),
                             kt_d[lb, :, hs]).then_inc(kt_in[half], 16)

            def load_v(c, half):
                lb = index(c // CPB)
                need(sp, pv_done, PAIRS * (c - 1) + 4 * (half + 1))
                cs = slice(half * 512, (half + 1) * 512)
                sp.dma_start(v[:, cs], v_d[lb, :, cs]).then_inc(v_in[half], 16)

            def load_res(c, t, layer):
                need(sp, y_out[t], 16 * c)
                src = xT if layer == 0 else x1_d
                sp.dma_start(res[:, t, :], src[t * P:(t + 1) * P, bass.ds((c - layer * NCH + 1) * Q - Q, Q)]).then_inc(r_in[t], 16)

            sp.wait_ge(c_split, 4)
            load_x(0, 0)
            sp.wait_ge(k_out, 16 * K_STORES * LAYERS)
            sp.wait_ge(ext_out, 16 * LAYERS * B)
            load_k(0, 0)
            load_k(0, 1)
            sp.wait_ge(v_out, 16 * B * LAYERS)
            load_v(0, 0)
            load_v(0, 1)
            sp.wait_ge(sup_out, 16 * 4)
            sp.wait_ge(pool_c, POOL_CONSTS)
            load_sup(0)
            sp.wait_ge(w_lo_done, KV + EXTRA)

            def step(g, s, layer):
                inside = not isinstance(g, int)
                nxt = inside or g + 1 < TOTAL
                here = inside or 0 <= g < TOTAL
                before = inside or g >= 1
                if here and nxt:
                    if s == 0:
                        load_x(g + 1, layer_of(g + 1, layer))
                    if s == 5:
                        load_sup(g + 1)
                    if s == 4:
                        load_k(g + 1, 0)
                    if s == 5:
                        load_v(g + 1, 0)
                if here and before:
                    if s == 0:
                        load_k(g, 1)
                    if s == 1:
                        load_v(g, 1)
                if before and s == 0:
                    load_res(g - 1, XT - 1, layer_of(g - 1, layer))
                if here and s >= 5:
                    load_res(g, s - 5, layer_of(g, layer))
                if here and isinstance(g, int):
                    if g == NCH - 1:
                        need(sp, sl_lo[0], s - 1)
                        sp.dma_start(w_st[:, s % 2, :, :], Wq[1, :, s * P:(s + 1) * P].rearrange("(k p) n -> p k n", p=P))\
                          .then_inc(sl_in[0][s % 2], 16)
                    if g == NCH:
                        if s == 0:
                            sp.wait_ge(sl_lo[0], PAIRS)
                        need(sp, sl_lo[1], s - 1)
                        hf, t = s // 4, s % 4
                        src = Wo[1, hf * 4 * P:(hf + 1) * 4 * P, t * P:(t + 1) * P]
                        sp.dma_start(w_st[:, s % 2, :, :], src.rearrange("(k p) n -> p k n", p=P)).then_inc(sl_in[1][s % 2], 16)
                if before and s >= 4:
                    t, c, lc = s - 4, g - 1, layer_of(g - 1, layer)
                    dst = yT if lc == LAYERS - 1 else x1_d
                    sp.wait_ge(res_done, PAIRS * c + s + 1)
                    sp.dma_start(dst[t * P:(t + 1) * P, bass.ds((c - lc * NCH + 1) * Q - Q, Q)], res[:, t, :]).then_inc(y_out[t], 16)

            chunks(sp, step)
            for t in range(XT):
                sp.wait_ge(y_out[t], 16 * TOTAL)

        @block.tensor
        def _(pe):
            pe.wait_ge(c_split, 4)
            for l in range(LAYERS):
                for w in range(W_TILES):
                    n, kk, sl = l * W_TILES + w, w % KTL, w % 4
                    pe.wait_ge(w_lo_done, n + 1)
                    parts = ((s_hi[sl], c_hi), (s_lo[sl], c_hi), (s_hi[sl], c_lo))
                    if w < KTL:
                        if w == 0 and l:
                            pe.wait_ge(k_lo_done, 4 * l)
                        for m in range(PAIRS):
                            for i, (wt, cx) in enumerate(parts):
                                mm = pe.matmul(banks[m // 2][:, (m % 2) * BT:(m % 2 + 1) * BT],
                                               wt[:, m * P:(m + 1) * P], cx[:, kk, :],
                                               start=(kk == 0 and i == 0 and m % 2 == 0),
                                               stop=(kk == KTL - 1 and i == 2), skip_group_check=True)
                    else:
                        if w == KTL and l:
                            pe.wait_ge(v_done, 4 * l)
                        for b in range(B):
                            for nh in range(2):
                                for i, (wt, cx) in enumerate(parts):
                                    mm = pe.matmul(banks[4 + 2 * b + nh][:, :], cx[:, kk, b * T:(b + 1) * T],
                                                   wt[:, nh * 512:(nh + 1) * 512],
                                                   start=(kk == 0 and i == 0), stop=(kk == KTL - 1 and i == 2))
                    mm.then_inc(w_used, 1)
            pe.wait_ge(k_lo_done, 4 * LAYERS)
            pe.wait_ge(v_done, 4 * LAYERS)
            pe.wait_ge(w_lo_done, KV + EXTRA)
            pe.wait_ge(consts, DVE_CONSTS)
            pe.wait_ge(pool_c, POOL_CONSTS)

            def logits(k, c, i):
                if i % 4 == 0:
                    pe.wait_ge(kt_in[i // 4], 16 * (c + 1))
                pe.wait_ge(qdup_done, k + 1)
                for h in range(2):
                    pe.wait_ge(qlo_done, 2 * k + h + 1)
                    pe.wait_ge(mrow_done, 2 * k + h + 1)
                    need(pe, p_done, 2 * k + h - 1)
                    hd = 2 * i + h
                    pe.matmul(lg_ps[h][:, :], km[:, hd, :], qe[:, i % 2, h, :], start=True, stop=False)
                    pe.matmul(lg_ps[h][:, :], kt[:, hd, :], qt[:, i % 2, h, :], start=False, stop=True)\
                      .then_inc(lg_done, 1)

            def spread(k, c, i):
                if i % 4 == 0:
                    pe.wait_ge(rec_done, 2 * c + i // 4 + 1)
                need(pe, on_done, k)
                pe.matmul(bc_ps[:, :], rsel[:, i % 4, :], rec_hi[:, :], start=True, stop=False)
                pe.matmul(bc_ps[:, :], rsel[:, i % 4, :], rec_lo[:, :], start=False, stop=True).then_inc(bc_done, 1)

            def maxima(k, c, i, h):
                if i % 4 == 0 and h == 0:
                    pe.wait_ge(km_in[i // 4], 32 * (c + 1))
                if h == 0:
                    pe.wait_ge(mz_done, 2 * k + 2)
                    need(pe, mrow_done, 2 * k)
                else:
                    need(pe, p_done, 2 * k)
                pe.wait_ge(qhi_done, 2 * k + h + 1)
                for n in range(NB):
                    mm = pe.matmul(mx_ps[h][:, n * T:(n + 1) * T], qe[:, i % 2, h, n * P:(n + 1) * P],
                                   km[:, 2 * i + h, :], start=True, stop=True)
                mm.then_inc(mx_done, 1)

            def turn_maxima(k, c, i):
                pe.wait_ge(mred_done, 2 * k + 2)
                for n in range(NB):
                    mm = pe.transpose(mx_ps[0][0:32, n * P:(n + 1) * P], mneg[:, i % 2, n, :], ident[:, :])
                mm.then_inc(mt_done, 1)

            def probs_v(k, c, i):
                if i % 4 == 0:
                    pe.wait_ge(v_in[i // 4], 16 * (c + 1))
                pe.wait_ge(p_done, 2 * k + 2)
                need(pe, oun_done, k)
                for h in range(2):
                    hd = 2 * i + h
                    mm = pe.matmul(pv_ps[h * D:(h + 1) * D, :], v[:, hd * D:(hd + 1) * D], probs[:, i % 4, h, :],
                                   start=True, stop=True)
                mm.then_inc(pv_done, 1)

            def denominators(k, c, i):
                rnd = (i // 2) % 2
                if rnd == 0:
                    need(pe, rec_raw, 2 * c + i // 4)
                for j in range(4):
                    mm = pe.matmul(sum_ps[32 * j:32 * j + 32, :], ssel[:, rnd, :], probs[:, (i - 1 + j // 2) % 4, j % 2, :],
                                   start=(rnd == 0), stop=(rnd == 1), skip_group_check=True)
                mm.then_inc(sum_done, 1)

            def project_q(k, c, i):
                if i == 0:
                    pe.wait_ge(x_hi_done, XT * (c + 1))
                if isinstance(c, int) and c == NCH:
                    pe.wait_ge(sl_lo[0], i + 1)
                need(pe, qhi_done, 2 * k)
                need(pe, qlo_done, 2 * k)
                n = 0
                for wt, xx in ((wq_hi, x_hi), (wq_lo, x_hi), (wq_hi, x_lo)):
                    if i == 0 and xx is x_lo:
                        pe.wait_ge(x_lo_done, XT * (c + 1))
                    for t in range(XT):
                        mm = pe.matmul(q_ps[:, :], wt[:, i, t, :], xx[:, t, :], start=(n == 0), stop=(n == 3 * XT - 1))
                        n += 1
                mm.then_inc(q_done, 1)

            def project_out(k, c, i, tiles, lc):
                hf, t = i // 4, i % 4
                if tiles[0] == 0:
                    if lc:
                        pe.wait_ge(sl_lo[1], i + 1)
                    need(pe, res_done, k)
                for kk in tiles:
                    if t == 0:
                        pe.wait_ge(o_done, PAIRS * c + 4 * hf + kk + 1)
                    for n, (wt, oo) in enumerate(((wo_hi, o_hi), (wo_lo, o_hi), (wo_hi, o_lo))):
                        mm = pe.matmul(out_ps[:, :], wt[:, hf, t, kk, :], oo[:, 4 * hf + kk, :],
                                       start=(kk == 0 and n == 0), stop=(kk == 3 and n == 2))
                if tiles[-1] == 3:
                    mm.then_inc(out_done, 1)

            def step(g, s, layer):
                now, ahead, far = pair(g, s, 0), pair(g, s, 1), pair(g, s, AHEAD)
                last, norm, unit = pair(g, s, -1), pair(g, s, -NORM), pair(g, s, -PAIRS)
                if now:
                    logits(*now)
                if last:
                    probs_v(*last)
                    if last[2] % 2:
                        denominators(*last)
                if ahead:
                    maxima(*ahead, 0)
                if norm:
                    spread(*norm)
                if ahead:
                    maxima(*ahead, 1)
                if unit:
                    project_out(*unit, range(3), layer_of(unit[1], layer))
                if ahead:
                    turn_maxima(*ahead)
                if unit:
                    project_out(*unit, range(3, 4), layer_of(unit[1], layer))
                if far:
                    project_q(*far)

            chunks(pe, step)

        @block.scalar
        def _(act):
            act.wait_ge(c_in, 16)
            nc.scalar.copy(c_hi[:, 0:4, :], c_f[:, 0:4, :]).then_inc(c_split, 1)
            nc.scalar.copy(c_hi[:, 4:8, :], c_f[:, 4:8, :]).then_inc(c_split, 1)
            for n in range(KV + EXTRA):
                l, w, sl = n // W_TILES, n % W_TILES, n % 4
                act.wait_ge(w_in[sl], 16 * (n // 4 + 1))
                if n < KV:
                    need(act, w_used, n - 3)
                    nc.scalar.copy(s_hi[sl], stage[sl]).then_inc(w_hi_done, 1)
                else:
                    j = n - KV
                    if j < 4:
                        dst = wq_hi[:, :, j, :]
                        src = stage[sl].rearrange("p (m c) -> p m c", c=P)
                    else:
                        dst = wo_hi[:, (j - 4) // 2, :, 2 * (j % 2):2 * (j % 2) + 2, :]
                        src = stage[sl].rearrange("p (a t c) -> p t a c", a=2, c=P)
                    nc.scalar.copy(dst, src).then_inc(w_hi_done, 1)
                if n < KV and w == KTL + 1:
                    act.wait_ge(w_used, l * W_TILES + KTL)
                    if l:
                        act.wait_ge(k_out, 16 * K_STORES * l)
                    for m in range(4):
                        nc.scalar.mul(k_hi[:, m * 512:(m + 1) * 512], banks[m][:, :], SCALE).then_inc(k_hi_done, 1)
                if n in (W_TILES + 1, KV + 1):
                    lv = n // W_TILES - 1
                    act.wait_ge(w_used, (lv + 1) * W_TILES)
                    if lv:
                        act.wait_ge(v_out, 16 * B * lv)
                    for m in range(4):
                        nc.scalar.copy(v_s[:, m // 2, (m % 2) * 512:(m % 2 + 1) * 512], banks[4 + m][:, :]).then_inc(v_done, 1)
                    act.wait_ge(v_done, 4 * (lv + 1))
                    for b in range(B):
                        act.dma_start(v_d[lv * B + b, :, :], v_s[:, b, :]).then_inc(v_out, 16)
            act.wait_ge(k_out, 16 * K_STORES * LAYERS)
            act.wait_ge(v_out, 16 * B * LAYERS)
            act.wait_ge(w_used, KV)
            act.wait_ge(w_lo_done, KV + EXTRA)

            def q_hi(k, c, i):
                act.wait_ge(q_done, k + 1)
                for h in range(2):
                    need(act, lg_done, 2 * k + h - 3)
                    nc.scalar.copy(qe[0:D, i % 2, h, :], q_ps[h * D:(h + 1) * D, :]).then_inc(qhi_done, 1)

            def exps(k, c, i):
                need(act, sum_done, PAIRS // 2 * c + i // 2 - 1)
                for h in range(2):
                    act.wait_ge(lg_done, 2 * k + h + 1)
                    nc.scalar.activation(probs[:, i % 4, h, :], lg_ps[h][:, :], ACT.Exp).then_inc(p_done, 1)

            def q_dup(k, c, i):
                act.wait_ge(qhi_done, 2 * k + 2)
                nc.scalar.copy(qt[0:D, i % 2, :, :], qe[0:D, i % 2, :, :]).then_inc(qdup_done, 1)

            def copy_o(k, c, i):
                act.wait_ge(pv_done, k + 1)
                need(act, o_done, k - 3)
                nc.scalar.copy(o_f[:, i % 4, :], pv_ps[:, :]).then_inc(oun_done, 1)

            def max_rows(k, c, i):
                act.wait_ge(mt_done, k + 1)
                for h in range(2):
                    nc.scalar.copy(qe[MRW:P, i % 2, h, :], mx_ps[0][0:32, :]).then_inc(mrow_done, 1)

            def split_x(c):
                act.wait_ge(x_in, 16 * (c + 1))
                need(act, q_done, PAIRS * c)
                for t in range(XT):
                    nc.scalar.copy(x_hi[:, t, :], x_f[:, t, :]).then_inc(x_hi_done, 1)

            def slice_hi(which, n, slot, dst, s_used, used):
                act.wait_ge(sl_in[which][slot], 16 * (n // 2 + 1))
                act.wait_ge(s_used, used)
                nc.scalar.copy(dst, w_st[:, slot, :, :]).then_inc(sl_hi[which], 1)

            split_x(0)

            def step(g, s, layer):
                now, ahead, last = pair(g, s, 0), pair(g, s, 1), pair(g, s, -1)
                if ahead:
                    q_hi(*ahead)
                if now:
                    exps(*now)
                if ahead:
                    q_dup(*ahead)
                if s == 6 and (not isinstance(g, int) or 0 <= g < TOTAL - 1):
                    split_x(g + 1)
                if ahead:
                    max_rows(*ahead)
                if last:
                    copy_o(*last)
                if isinstance(g, int) and g == NCH - 1:
                    slice_hi(0, s, s % 2, wq_hi[:, s, :, :], q_done, PAIRS * g + s + 1)
                if isinstance(g, int) and g == NCH:
                    for n in ([s - 1] if s else []) + ([s] if s == PAIRS - 1 else []):
                        slice_hi(1, n, n % 2, wo_hi[:, n // 4, n % 4, :, :], out_done, PAIRS * (g - 1) + n + 1)

            chunks(act, step)

        @block.vector
        def _(dve):
            chain = [0]

            def link(ins):
                chain[0] += 1
                ins.then_inc(consts, 1)
                dve.wait_ge(consts, chain[0])

            dve.wait_ge(c_split, 2)
            for i in range(2):
                nc.vector.tensor_tensor(c_lo[:, 4 * i:4 * i + 4, :], c_f[:, 4 * i:4 * i + 4, :],
                                        c_hi[:, 4 * i:4 * i + 4, :], ALU.subtract).then_inc(c_split, 1)

            def bias_rows():
                dve.wait_ge(small_in, 16 * 3)
                rows = m_f
                link(nc.vector.tensor_scalar(rows, rows, -1.0, 1.0, ALU.mult, ALU.add))
                link(nc.vector.tensor_scalar(rows, rows, -SUPPRESS / 2, None, ALU.mult))
                link(nc.vector.tensor_copy(m_hi, rows))
                link(nc.vector.tensor_tensor(m_lo, rows, m_hi, ALU.subtract))

            def const_tables():
                dve.wait_ge(pool_c, 2)
                link(nc.vector.tensor_copy(idx_f, ints[:, 0:2 * LAYERS * NI]))
                link(nc.vector.tensor_copy(tok[:, 0:T], ints[:, 64:64 + T]))
                link(nc.vector.tensor_copy(row_s[:, 0:1], ints[:, 32:33]))
                link(nc.vector.tensor_scalar(idx_w, idx_f, float(T), None, ALU.add))
                link(nc.vector.tensor_scalar(ident[:, :], tok[:, 0:P], row_s[:, 0:1], None, ALU.is_equal))

                def is_row(dst, lo, hi):
                    link(nc.vector.tensor_scalar(dst, row_s[:, 0:1], float(lo), None, ALU.is_ge))
                    link(nc.vector.scalar_tensor_tensor(out=dst, in0=row_s[:, 0:1], scalar=float(hi), in1=dst,
                                                        op0=ALU.is_lt, op1=ALU.mult))
                for n, lo in enumerate((SUP, SUP + 2)):
                    is_row(row_s[:, 1 + n:2 + n], lo, lo + 2)
                for h in range(2):
                    is_row(row_s[:, 3 + h:4 + h], MRW + h, MRW + h + 1)
                for n in range(4):
                    for h in range(2):
                        r = 32 * (2 * (n % 2) + h) + n // 2
                        c0 = 5 + 2 * n + h
                        is_row(row_s[:, c0:c0 + 1], r, r + 1)
                        link(nc.vector.tensor_scalar(rsel[:, n, h * D:(h + 1) * D], tok[:, 0:D], 0.0,
                                                     row_s[:, c0:c0 + 1], ALU.mult, ALU.add))
                for l in range(LAYERS):
                    for a, dst in enumerate((ind_a, ind_b)):
                        link(nc.vector.memset(dst, 0.0))
                        for n in range(NI):
                            at = (2 * l + a) * NI + n
                            for col in (idx_f, idx_w):
                                link(nc.vector.scalar_tensor_tensor(out=dst, in0=tok[:, 0:T], scalar=col[:, at:at + 1],
                                                                    in1=dst, op0=ALU.is_equal, op1=ALU.max))
                    link(nc.vector.tensor_scalar(ind_n, ind_b, -1.0, 1.0, ALU.mult, ALU.add))
                    link(nc.vector.tensor_tensor(ind_a, ind_a, ind_n, ALU.mult))
                    for h in range(2):
                        link(nc.vector.tensor_scalar(ind_n, ind_a, row_s[:, 1:2], row_s[:, 3 + h:4 + h], ALU.mult, ALU.add))
                        link(nc.vector.scalar_tensor_tensor(out=ext[:, l, h, :], in0=ind_b, scalar=row_s[:, 2:3], in1=ind_n,
                                                            op0=ALU.mult, op1=ALU.add))

            for n in range(KV + EXTRA):
                l, w, sl = n // W_TILES, n % W_TILES, n % 4
                dve.wait_ge(w_hi_done, n + 1)
                if n < KV:
                    nc.vector.tensor_tensor(s_lo[sl], stage[sl], s_hi[sl], ALU.subtract).then_inc(w_lo_done, 1)
                else:
                    j = n - KV
                    if j < 4:
                        dst, hi = wq_lo[:, :, j, :], wq_hi[:, :, j, :]
                        src = stage[sl].rearrange("p (m c) -> p m c", c=P)
                        nc.vector.tensor_tensor(dst, src, hi, ALU.subtract).then_inc(w_lo_done, 1)
                    else:
                        a0 = 2 * (j % 2)
                        dst = wo_lo[:, (j - 4) // 2, :, a0:a0 + 2, :]
                        hi = wo_hi[:, (j - 4) // 2, :, a0:a0 + 2, :]
                        src = stage[sl].rearrange("p (a t c) -> p t a c", a=2, c=P)
                        nc.vector.tensor_tensor(dst, src, hi, ALU.subtract).then_inc(w_lo_done, 1)
                if n == 3:
                    bias_rows()
                if n == 5:
                    const_tables()
                if n < KV and w == KTL + 1:
                    for m in range(4):
                        dve.wait_ge(k_hi_done, 4 * l + m + 1)
                        nc.vector.scalar_tensor_tensor(out=k_lo[:, m * 512:(m + 1) * 512], in0=banks[m][:, :], scalar=SCALE,
                                                       in1=k_hi[:, m * 512:(m + 1) * 512], op0=ALU.mult,
                                                       op1=ALU.subtract).then_inc(k_lo_done, 1)
            assert chain[0] == DVE_CONSTS, chain[0]
            dve.wait_ge(k_out, 16 * K_STORES * LAYERS)

            def q_lo(k, c, i):
                for h in range(2):
                    dve.wait_ge(qhi_done, 2 * k + h + 1)
                    need(dve, lg_done, 2 * k + h - 3)
                    nc.vector.tensor_tensor(qt[D:P, i % 2, h, :], q_ps[h * D:(h + 1) * D, :], qe[0:D, i % 2, h, :],
                                            ALU.subtract).then_inc(qlo_done, 1)

            def row_max(k, c, i, h):
                dve.wait_ge(mx_done, 2 * k + h + 1)
                if h == 0:
                    need(dve, mt_done, k - 1)
                nc.vector.tensor_reduce(mneg[:, i % 2, :, h], mx_ps[h][:, :].rearrange("p (n t) -> p n t", t=T), AX_X,
                                        ALU.max, negate=True).then_inc(mred_done, 1)

            def normalise(k, c, i):
                dve.wait_ge(bc_done, k + 1)
                dve.wait_ge(oun_done, k + 1)
                nc.vector.tensor_tensor(o_f[:, i % 4, :], o_f[:, i % 4, :], bc_ps[:, :], ALU.mult).then_inc(on_done, 1)

            def split_o(k, c, i):
                need(dve, out_done, PAIRS * c + 4 * (i // 4) - 4)
                dve.wait_ge(on_done, k + 1)
                nc.vector.tensor_copy(o_hi[:, i, :], o_f[:, i % 4, :]).then_inc(oh_done, 1)
                dve.wait_ge(oh_done, k + 1)
                nc.vector.tensor_tensor(o_lo[:, i, :], o_f[:, i % 4, :], o_hi[:, i, :], ALU.subtract).then_inc(o_done, 1)

            def reciprocals(k, c, i):
                n = 2 * c + i // 4
                dve.wait_ge(sum_done, 2 * n + 2)
                nc.vector.reciprocal(rec[:, :], sum_ps[:, :]).then_inc(rec_raw, 1)
                need(dve, bc_done, 4 * n)
                dve.wait_ge(rec_raw, n + 1)
                nc.vector.tensor_copy(rec_hi[:, :], rec[:, :]).then_inc(rec_h, 1)
                dve.wait_ge(rec_h, n + 1)
                nc.vector.tensor_tensor(rec_lo[:, :], rec[:, :], rec_hi[:, :], ALU.subtract).then_inc(rec_done, 1)

            def add_out(k, c, i, lc):
                hf, t = i // 4, i % 4
                dve.wait_ge(out_done, k + 1)
                if hf == 0:
                    dve.wait_ge(r_in[t], 16 * (c + 1))
                    ins = nc.vector.scalar_tensor_tensor(out=res[:, t, :], in0=out_ps[:, :], scalar=bo_s[:, lc, t:t + 1],
                                                         in1=res[:, t, :], op0=ALU.add, op1=ALU.add)
                else:
                    dve.wait_ge(res_done, k - 3)
                    ins = nc.vector.tensor_tensor(res[:, t, :], out_ps[:, :], res[:, t, :], ALU.add)
                ins.then_inc(res_done, 1)

            def split_x(c):
                for t in range(XT):
                    dve.wait_ge(x_hi_done, XT * c + t + 1)
                    nc.vector.tensor_tensor(x_lo[:, t, :], x_f[:, t, :], x_hi[:, t, :], ALU.subtract).then_inc(x_lo_done, 1)

            def slice_lo(which, n, slot, dst, hi):
                dve.wait_ge(sl_hi[which], n + 1)
                nc.vector.tensor_tensor(dst, w_st[:, slot, :, :], hi, ALU.subtract).then_inc(sl_lo[which], 1)

            split_x(0)

            def step(g, s, layer):
                ahead, last, norm, unit = pair(g, s, 1), pair(g, s, -1), pair(g, s, -NORM), pair(g, s, -PAIRS)
                if ahead:
                    q_lo(*ahead)
                    row_max(*ahead, 0)
                    row_max(*ahead, 1)
                if s == 6 and (not isinstance(g, int) or 0 <= g < TOTAL - 1):
                    split_x(g + 1)
                if norm:
                    normalise(*norm)
                    split_o(*norm)
                if last and last[2] % 4 == 3:
                    reciprocals(*last)
                if unit:
                    add_out(*unit, layer_of(unit[1], layer))
                if isinstance(g, int) and g == NCH - 1:
                    slice_lo(0, s, s % 2, wq_lo[:, s, :, :], wq_hi[:, s, :, :])
                if isinstance(g, int) and g == NCH:
                    for n in ([s - 1] if s else []) + ([s] if s == PAIRS - 1 else []):
                        slice_lo(1, n, n % 2, wo_lo[:, n // 4, n % 4, :, :], wo_hi[:, n // 4, n % 4, :, :])

            chunks(dve, step)

        @block.gpsimd
        def _(pool):
            nc.gpsimd.iota(ints[:, 64:64 + T], pattern=[[1, T]], base=0, channel_multiplier=0).then_inc(pool_c, 1)
            nc.gpsimd.iota(ints[:, 32:33], pattern=[[0, 1]], base=0, channel_multiplier=1).then_inc(pool_c, 1)
            nc.gpsimd.memset(mneg[:, :, :, :], 0.0).then_inc(pool_c, 1)
            for r in range(2):
                nc.gpsimd.memset(ssel[:, r, 0:1], 1.0 - r).then_inc(pool_c, 1)
                nc.gpsimd.memset(ssel[:, r, 1:2], float(r)).then_inc(pool_c, 1)
                nc.gpsimd.memset(ssel[:, r, 2:32], 1.0 - r).then_inc(pool_c, 1)
            pool.wait_ge(consts, DVE_CONSTS)
            for l in range(LAYERS):
                for b in range(B):
                    rows = km_d[l * B + b, SUP:P, :].rearrange("p (m n) -> p m n", m=PAIRS)
                    src = ext[SUP:P, l, :, :].bitcast(F32).rearrange("p a t -> p (a t)").unsqueeze(1).to_broadcast([P - SUP, PAIRS, 2 * T])
                    pool.dma_start(rows, src).then_inc(ext_out, 16)
            pool.wait_ge(ext_out, 16 * LAYERS * B)
            pool.wait_ge(pool_c, POOL_CONSTS - 1)
            nc.gpsimd.memset(sup_c[SUP:P, :].bitcast(F32), 0.0).then_inc(pool_c, 1)
            pool.wait_ge(pool_c, POOL_CONSTS)
            pool.wait_ge(k_out, 16 * K_STORES * LAYERS)

            def rows(k, c, i):
                need(pool, lg_done, 2 * k - 2)
                if i == 0:
                    pool.wait_ge(sup_in, 16 * (c + 1))
                for h in range(2):
                    src = sup_c[SUP:P, :].bitcast(F32)
                    nc.gpsimd.tensor_tensor(qe[SUP:P, i % 2, h, :], src, src, ALU.add).then_inc(mz_done, 1)

            def step(g, s, layer):
                far = pair(g, s, AHEAD)
                if far:
                    rows(*far)

            chunks(pool, step)


def kernel(**inputs):
    import numpy as np
    import concourse.bacc as bacc
    from concourse.bass_utils import run_bass_kernel_spmd

    a = {k: np.asarray(x) for k, x in inputs.items()}
    Bn, HWn, Cn = a["x"].shape
    lay = ("L0_xattn_", "L1_xattn_")
    arrays = {
        "xT": np.ascontiguousarray(a["x"].reshape(Bn * HWn, Cn).T),
        "ctxT": np.ascontiguousarray(a["ctx_2048"].reshape(-1, a["ctx_2048"].shape[-1]).T),
        "masks": np.stack([a["mask_S_fk1"], a["mask_S_fk0"]]),
        "Wk": np.stack([a[l + "Wk"] for l in lay]),
        "Wv": np.stack([a[l + "Wv"] for l in lay]),
        "Wq": np.stack([a[l + "Wq"] for l in lay]),
        "Wo": np.stack([a[l + "Wo"] for l in lay]),
        "bo": np.ascontiguousarray(np.stack([a[l + "bo"] for l in lay]).reshape(-1, P).T),
        "idx": np.concatenate([a[l + "token_indices_" + s] for l in lay for s in "AB"])[None, :],
    }
    nc = bacc.Bacc("TRN2", target_bir_lowering=False, num_devices=1)
    args = [nc.dram_tensor(n, x.shape, mybir.dt.from_np(x.dtype), kind="ExternalInput").ap() for n, x in arrays.items()]
    yT = nc.dram_tensor("yT", (Cn, Bn * HWn), F32, kind="ExternalOutput").ap()
    two_cross_attentions(nc, *args, yT)
    r = run_bass_kernel_spmd(nc, [arrays], core_ids=[0])
    return np.ascontiguousarray(r.results[0]["yT"].T).reshape(Bn, HWn, Cn)
```

```python
from contextlib import ExitStack

import concourse.bass as bass
from concourse import mybir

F32 = mybir.dt.float32
F32R = mybir.dt.float32r
I32 = mybir.dt.int32
ALU = mybir.AluOpType
ACT = mybir.ActivationFunctionType
AX_X = mybir.AxisListType.X

P = 128
LAYERS = 2
SUPPRESS = 20.0


def two_cross_attentions(nc, xT, ctxT, masks, Wk, Wv, Wq, Wo, bo, idx, yT):
    C, ROWS = xT.shape
    CT, BT = ctxT.shape
    HW = masks.shape[1]
    INNER = Wk.shape[2]
    B = ROWS // HW
    T = BT // B
    NI = idx.shape[1] // (2 * LAYERS)
    D = 64
    H = INNER // D
    PAIRS = H // 2
    Q = 512
    NCH = ROWS // Q
    CPB = HW // Q
    TOTAL = LAYERS * NCH
    XT = C // P
    KTL = CT // P
    NB = Q // P
    SCALE = float(D) ** -0.5
    SUP = 64
    MRW = 96
    AHEAD = 2
    NORM = 5
    assert T == P and PAIRS == 8 and XT == 4 and NB == 4 and NCH == 8 and B == 2

    kh_d = nc.dram_tensor("kh_d", (LAYERS * B, P, PAIRS * T), F32, kind="Internal").ap()
    kl_d = nc.dram_tensor("kl_d", (LAYERS * B, P, PAIRS * T), F32, kind="Internal").ap()
    ext_d = nc.dram_tensor("ext_d", (LAYERS, P - SUP, 2 * T), F32, kind="Internal").ap()
    v_d = nc.dram_tensor("v_d", (LAYERS * B, T, INNER), F32, kind="Internal").ap()
    sup_d = nc.dram_tensor("sup_d", (4, HW), F32, kind="Internal").ap()
    x1_d = nc.dram_tensor("x1_d", (C, ROWS), F32, kind="Internal").ap()

    with ExitStack() as ctx:
        def sb(name, shape, dt):
            return ctx.enter_context(nc.sbuf_tensor(name, shape, dt))

        def sem(name):
            return ctx.enter_context(nc.semaphore(name))

        wq_hi = sb("wq_hi", [P, PAIRS, XT, P], F32R)
        wq_lo = sb("wq_lo", [P, PAIRS, XT, P], F32R)
        wo_hi = sb("wo_hi", [P, 2, XT, 4, P], F32R)
        wo_lo = sb("wo_lo", [P, 2, XT, 4, P], F32R)
        km = sb("km", [P, H, T], F32R)
        kt = sb("kt", [P, H, T], F32R)
        v = sb("v", [P, INNER], F32)
        x_f = sb("x_f", [P, XT, Q], F32)
        x_hi = sb("x_hi", [P, XT, Q], F32R)
        x_lo = sb("x_lo", [P, XT, Q], F32R)
        qe = sb("qe", [P, 2, 2, Q], F32R)
        qt = sb("qt", [P, 2, 2, Q], F32R)
        probs = sb("probs", [P, 2, 2, Q], F32)
        fold = sb("fold", [P, 4, Q], F32)
        o_f = sb("o_f", [P, 4, Q], F32)
        o_hi = sb("o_hi", [P, 8, Q], F32R)
        o_lo = sb("o_lo", [P, 8, Q], F32R)
        res = sb("res", [P, XT, Q], F32)
        w_st = sb("w_st", [P, 2, 4, P], F32)
        rec = sb("rec", [P, Q], F32)
        rec_s = sb("rec_s", [P, 2, Q], F32R)
        sup_c = sb("sup_c", [P, Q], F32R)
        mneg = sb("mneg", [P, 2, NB, 32], F32)
        ident = sb("ident", [P, P], F32)
        rsel = sb("rsel", [P, 2, P], F32R)
        ssel = sb("ssel", [P, 32], F32)
        bo_s = sb("bo_s", [P, LAYERS, XT], F32)

        c_f = x_f[:, :, :].rearrange("p a (b n) -> p (a b) n", n=BT)
        c_hi = wo_hi[:, 0, :, :, :].rearrange("p a b n -> p (a b n)").rearrange("p (k n) -> p k n", n=BT)
        c_lo = wo_lo[:, 0, :, :, :].rearrange("p a b n -> p (a b n)").rearrange("p (k n) -> p k n", n=BT)
        stage = [res[:, 0:2, :], res[:, 2:4, :], o_f[:, 0:2, :], o_f[:, 2:4, :]]
        stage = [s.rearrange("p a b -> p (a b)") for s in stage]
        s_hi = [o_hi[:, 2 * i:2 * i + 2, :].rearrange("p a b -> p (a b)") for i in range(4)]
        s_lo = [o_lo[:, 2 * i:2 * i + 2, :].rearrange("p a b -> p (a b)") for i in range(4)]
        k_hi = qt[:, :, :, :].rearrange("p a b n -> p (a b n)")
        k_lo = qe[:, :, :, :].rearrange("p a b n -> p (a b n)")
        v_s = probs[:, :, :, :].rearrange("p b n c -> p b (n c)")
        tok = rec
        ind = fold[:, 0:2, :].rearrange("p a n -> p (a n)")
        ind_a, ind_b, ind_n = (ind[:, i * T:(i + 1) * T] for i in range(3))
        idx_f = ind[:, 3 * T:3 * T + 2 * LAYERS * NI]
        idx_w = ind[:, 3 * T + 32:3 * T + 32 + 2 * LAYERS * NI]
        row_s = ind[:, 3 * T + 64:3 * T + 128]
        ints = fold[:, 2, :].bitcast(I32)
        ext = sup_c[:, :].rearrange("p (l a t) -> p l a t", l=LAYERS, a=2)
        MR = 2 * HW // P
        m_f, m_hi, m_lo = w_st[0:MR, 0, 0, :], rec_s[0:MR, 0, 0:P], rec_s[0:MR, 1, 0:P]

        banks = [ctx.enter_context(nc.psum_tensor(f"bank{i}", [P, 512], F32)) for i in range(8)]
        q_ps, bc_ps, out_ps = banks[0], banks[2], banks[3]
        lg_ps = [banks[4], banks[5]]
        mx_ps = [banks[1], lg_ps[1]]
        pv_ps, sum_ps = banks[6], banks[7]

        c_in = [sem(f"c_in{i}") for i in range(4)]
        c_hi_done = sem("c_hi_done")
        c_lo_done = sem("c_lo_done")
        w_in = [sem(f"w_in{i}") for i in range(4)]
        w_hi_done = sem("w_hi_done")
        w_lo_done = sem("w_lo_done")
        w_used = sem("w_used")
        k_hi_done = sem("k_hi_done")
        k_lo_done = sem("k_lo_done")
        k_out = sem("k_out")
        v_done = sem("v_done")
        v_out = sem("v_out")
        consts = sem("consts")
        pool_c = sem("pool_c")
        small_in = sem("small_in")
        sup_out = sem("sup_out")
        ext_out = sem("ext_out")
        x_in = sem("x_in")
        x_hi_done = sem("x_hi_done")
        x_lo_done = sem("x_lo_done")
        sup_in = sem("sup_in")
        km_in = [sem(f"km_in{i}") for i in range(2)]
        kt_in = [sem(f"kt_in{i}") for i in range(2)]
        v_in = [sem(f"v_in{i}") for i in range(2)]
        q_done = sem("q_done")
        qhi_done = sem("qhi_done")
        qlo_done = sem("qlo_done")
        qdup_done = sem("qdup_done")
        mz_done = sem("mz_done")
        mx_done = sem("mx_done")
        mred_done = sem("mred_done")
        mt_done = sem("mt_done")
        mrow_done = sem("mrow_done")
        lg_done = sem("lg_done")
        p_done = sem("p_done")
        pv_done = sem("pv_done")
        half_done = sem("half_done")
        fold_done = sem("fold_done")
        sum_done = sem("sum_done")
        oun_done = sem("oun_done")
        rec_raw = sem("rec_raw")
        rec_h = sem("rec_h")
        rec_done = sem("rec_done")
        bc_done = sem("bc_done")
        on_done = sem("on_done")
        oh_done = sem("oh_done")
        o_done = sem("o_done")
        out_done = sem("out_done")
        res_done = sem("res_done")
        r_in = [sem(f"r_in{i}") for i in range(XT)]
        y_out = [sem(f"y_out{i}") for i in range(XT)]
        sl_in = [[sem(f"{w}_sl_in{i}") for i in range(2)] for w in ("wq", "wo")]
        sl_hi = [sem("wq_sl_hi"), sem("wo_sl_hi")]
        sl_lo = [sem("wq_sl_lo"), sem("wo_sl_lo")]

        block = ctx.enter_context(nc.Block())

        W_TILES = 2 * KTL
        KV = LAYERS * W_TILES
        K_STORES = 2 * B
        TILES = []
        for n in range(KV):
            TILES.append((n // W_TILES, n % W_TILES))
            if n % 8 == 5:
                TILES.append((None, n // 8))
        BIAS_STEPS = 3 + 8 + 2 + 3 + 4
        DVE_CONSTS = BIAS_STEPS + 12 + LAYERS * (2 * NI + 2 + 4)
        POOL_CONSTS = 7

        def need(eng, s, count):
            if not isinstance(count, int) or count > 0:
                eng.wait_ge(s, count)

        def pair(g, s, off):
            i = s + off
            dg, i = i // PAIRS, i % PAIRS
            c = g + dg
            if isinstance(c, int) and not 0 <= c < TOTAL:
                return None
            return c * PAIRS + i, c, i

        def chunks(eng, step):
            for s in (6, 7):
                step(-1, s, 0)
            for layer in range(LAYERS):
                g0 = layer * NCH
                alone = range(2) if layer == 0 else range(g0, g0 + 1)
                for g in alone:
                    for s in range(PAIRS):
                        step(g, s, layer)
                with eng.Fori(alone[-1] + 1, g0 + NCH - 1) as g:
                    for s in range(PAIRS):
                        step(g, s, layer)
                for s in range(PAIRS):
                    step(g0 + NCH - 1, s, layer)
            for s in range(PAIRS):
                step(TOTAL, s, LAYERS - 1)

        def final(c):
            return isinstance(c, int) and c == TOTAL - 1

        def out_bank(c, i):
            return (out_ps, q_ps, mx_ps[0], lg_ps[0], lg_ps[1])[i % 5] if final(c) else out_ps

        def bc_bank(c, i):
            return sum_ps if final(c) and i >= 4 and i % 2 else bc_ps

        def layer_of(g, layer):
            return g // NCH if isinstance(g, int) else layer

        @block.sync
        def _(sp):
            def w_load(n):
                need(sp, w_lo_done, n - 3)
                l, w = TILES[n]
                kk = w % KTL
                src = Wq[0, w * P:(w + 1) * P, :] if l is None else (Wk if w < KTL else Wv)[l, kk * P:(kk + 1) * P, :]
                sp.dma_start(stage[n % 4], src).then_inc(w_in[n % 4], 16)

            for i in range(4):
                ks = slice(2 * i, 2 * i + 2)
                sp.dma_start(c_f[:, ks, :], ctxT[2 * i * P:(2 * i + 2) * P, :].rearrange("(k p) n -> p k n", p=P))\
                  .then_inc(c_in[i], 16)
                w_load(i)

            def index(value):
                return value if isinstance(value, int) else sp.snap(value)

            def load_x(c, layer):
                need(sp, x_lo_done, XT * c)
                src = xT if layer == 0 else x1_d
                if layer:
                    for t in range(XT):
                        sp.wait_ge(y_out[t], 16 * (c - NCH + 1))
                col = (c - layer * NCH) * Q
                sp.dma_start(x_f[:, :, :], src[:, bass.ds(col, Q)].rearrange("(t p) n -> p t n", p=P)).then_inc(x_in, 16)

            def load_sup(c):
                at = index(c % CPB)
                need(sp, mz_done, 2 * PAIRS * c)
                sp.dma_start(sup_c[SUP:SUP + 4, :].bitcast(F32), sup_d[:, bass.ds(at * Q, Q)]).then_inc(sup_in, 16)

            def load_k(c, half, layer):
                lb = index(c // CPB)
                need(sp, lg_done, 2 * (PAIRS * (c - 1) + 4 * (half + 1)))
                heads = slice(half * 8, half * 8 + 8)
                ms = slice(half * 4 * T, (half + 1) * 4 * T)
                end = P if isinstance(c, int) and c == 0 else SUP + 4
                sp.dma_start(km[SUP:end, heads, :].rearrange("p (m h) t -> p m (h t)", h=2).bitcast(F32),
                             ext_d[layer, 0:end - SUP, :].unsqueeze(1).to_broadcast([end - SUP, PAIRS // 2, 2 * T]))\
                  .then_inc(km_in[half], 16)
                for dst, k_d, done in ((km[0:D, heads, :], kh_d, km_in), (kt[0:D, heads, :], kl_d, kt_in),
                                       (kt[D:P, heads, :], kh_d, kt_in)):
                    dst = dst.rearrange("d (m h) t -> d h m t", h=2).bitcast(F32)
                    for h in range(2):
                        sp.dma_start(dst[:, h, :, :], k_d[lb, h * D:(h + 1) * D, ms].rearrange("d (m t) -> d m t", t=T))\
                          .then_inc(done[half], 16)

            def load_v(c, half):
                lb = index(c // CPB)
                need(sp, pv_done, PAIRS * (c - 1) + 4 * (half + 1))
                cs = slice(half * 512, (half + 1) * 512)
                sp.dma_start(v[:, cs], v_d[lb, :, cs]).then_inc(v_in[half], 16)

            def load_res(c, t, layer):
                need(sp, y_out[t], 16 * c)
                src = xT if layer == 0 else x1_d
                sp.dma_start(res[:, t, :], src[t * P:(t + 1) * P, bass.ds((c - layer * NCH + 1) * Q - Q, Q)]).then_inc(r_in[t], 16)

            for n in range(4, len(TILES)):
                w_load(n)
                l, w = TILES[n]
                if n == 12:
                    sp.wait_ge(c_lo_done, 4)
                    load_x(0, 0)
                if n == 8:
                    sp.wait_ge(consts, BIAS_STEPS)
                    for i, part in enumerate((m_hi, m_lo)):
                        for a in range(2):
                            sp.dma_start(sup_d[2 * a + i, :].rearrange("(r n) -> r n", n=P),
                                         part[a * MR // 2:(a + 1) * MR // 2, :].bitcast(F32)).then_inc(sup_out, 16)
                if l is not None and w == W_TILES - 3:
                    for part, dst, split in ((k_hi, kh_d, k_hi_done), (k_lo, kl_d, k_lo_done)):
                        sp.wait_ge(split, 4 * (l + 1))
                        for b in range(B):
                            sp.dma_start(dst[l * B + b, :, :].rearrange("p (m t) -> p m t", t=T),
                                         part.rearrange("p (m b t) -> p m b t", b=B, t=T)[:, :, b, :].bitcast(F32))\
                              .then_inc(k_out, 16)
                if l == 1 and w == 3:
                    sp.wait_ge(k_out, 16 * K_STORES)
                    sp.wait_ge(ext_out, 16 * LAYERS)
                    load_k(0, 0, 0)
                if l == 1 and w == 5:
                    sp.wait_ge(v_out, 16)
                    load_v(0, 0)
                if l == 1 and w == 7:
                    sp.wait_ge(sup_out, 16 * 4)
                    sp.wait_ge(pool_c, POOL_CONSTS)
                    load_sup(0)
            load_k(0, 1, 0)
            load_v(0, 1)
            sp.wait_ge(k_out, 16 * K_STORES * LAYERS)
            sp.wait_ge(v_out, 16 * LAYERS)
            sp.wait_ge(w_lo_done, len(TILES))

            def step(g, s, layer):
                inside = not isinstance(g, int)
                nxt = inside or g + 1 < TOTAL
                here = inside or 0 <= g < TOTAL
                before = inside or g >= 1
                if here and nxt:
                    if s == 0:
                        load_x(g + 1, layer_of(g + 1, layer))
                    if s == 5:
                        load_sup(g + 1)
                    if s == 4:
                        load_k(g + 1, 0, layer_of(g + 1, layer))
                    if s == 5:
                        load_v(g + 1, 0)
                if here and before:
                    if s == 0:
                        load_k(g, 1, layer_of(g, layer))
                    if s == 1:
                        load_v(g, 1)
                if before and s == 0:
                    load_res(g - 1, XT - 1, layer_of(g - 1, layer))
                if here and s >= 5:
                    load_res(g, s - 5, layer_of(g, layer))
                if isinstance(g, int):
                    if g == NCH - 1:
                        need(sp, sl_lo[0], s - 1)
                        sp.dma_start(w_st[:, s % 2, :, :], Wq[1, :, s * P:(s + 1) * P].rearrange("(k p) n -> p k n", p=P))\
                          .then_inc(sl_in[0][s % 2], 16)
                    if g in (0, NCH):
                        l = g // NCH
                        if l and s == 0:
                            sp.wait_ge(sl_lo[0], PAIRS)
                        need(sp, sl_lo[1], l * PAIRS + s - 1)
                        hf, t = s // 4, s % 4
                        src = Wo[l, hf * 4 * P:(hf + 1) * 4 * P, t * P:(t + 1) * P]
                        sp.dma_start(w_st[:, s % 2, :, :], src.rearrange("(k p) n -> p k n", p=P)).then_inc(sl_in[1][s % 2], 16)
                if before and s >= 4:
                    t, c, lc = s - 4, g - 1, layer_of(g - 1, layer)
                    dst = yT if lc == LAYERS - 1 else x1_d
                    sp.wait_ge(res_done, PAIRS * c + s + 1)
                    sp.dma_start(dst[t * P:(t + 1) * P, bass.ds((c - lc * NCH + 1) * Q - Q, Q)], res[:, t, :]).then_inc(y_out[t], 16)

            chunks(sp, step)
            for t in range(XT):
                sp.wait_ge(y_out[t], 16 * TOTAL)

        @block.tensor
        def _(pe):
            for l in range(LAYERS):
                for w in range(W_TILES):
                    n, kk, sl = l * W_TILES + w, w % KTL, w % 4
                    if not l and w < KTL and w % 2 == 0:
                        pe.wait_ge(c_lo_done, w // 2 + 1)
                    pe.wait_ge(w_lo_done, TILES.index((l, w)) + 1)
                    parts = ((s_hi[sl], c_hi), (s_lo[sl], c_hi), (s_hi[sl], c_lo))
                    if w < KTL:
                        if w == 0 and l:
                            pe.wait_ge(k_lo_done, 4 * l)
                        for m in range(PAIRS):
                            for i, (wt, cx) in enumerate(parts):
                                mm = pe.matmul(banks[m // 2][:, (m % 2) * BT:(m % 2 + 1) * BT],
                                               wt[:, m * P:(m + 1) * P], cx[:, kk, :],
                                               start=(kk == 0 and i == 0 and m % 2 == 0),
                                               stop=(kk == KTL - 1 and i == 2), skip_group_check=True)
                    else:
                        if w == KTL and l:
                            pe.wait_ge(v_done, 4 * l)
                        for b in range(B):
                            for nh in range(2):
                                for i, (wt, cx) in enumerate(parts):
                                    mm = pe.matmul(banks[4 + 2 * b + nh][:, :], cx[:, kk, b * T:(b + 1) * T],
                                                   wt[:, nh * 512:(nh + 1) * 512],
                                                   start=(kk == 0 and i == 0), stop=(kk == KTL - 1 and i == 2))
                    mm.then_inc(w_used, 1)
            pe.wait_ge(k_lo_done, 4 * LAYERS)
            pe.wait_ge(w_lo_done, len(TILES))
            pe.wait_ge(consts, DVE_CONSTS)
            pe.wait_ge(pool_c, POOL_CONSTS)

            def logits(k, c, i):
                if i % 4 == 0:
                    pe.wait_ge(kt_in[i // 4], 64 * (c + 1))
                pe.wait_ge(qdup_done, k + 1)
                pe.wait_ge(qlo_done, 2 * k + 2)
                pe.wait_ge(mrow_done, NB * (k + 1))
                for h in range(2):
                    hd = 2 * i + h
                    pe.matmul(lg_ps[h][:, :], km[:, hd, :], qe[:, i % 2, h, :], start=True, stop=False)
                    pe.matmul(lg_ps[h][:, :], kt[:, hd, :], qt[:, i % 2, h, :], start=False, stop=True)\
                      .then_inc(lg_done, 1)

            def spread(k, c, i):
                if i % 2 == 0:
                    pe.wait_ge(rec_done, 2 * (2 * c + i // 4) + i // 2 % 2 + 1)
                need(pe, on_done, k - 1 if final(c) and i > 4 else k)
                pe.matmul(bc_bank(c, i)[:, :], rsel[:, i % 2, :], rec_s[:, (i // 2) % 2, :], start=True, stop=True).then_inc(bc_done, 1)

            def maxima(k, c, i, h):
                if i % 4 == 0 and h == 0:
                    pe.wait_ge(km_in[i // 4], 48 * (c + 1))
                if h == 0:
                    pe.wait_ge(mz_done, 2 * k + 2)
                elif isinstance(k, int) and k == 0:
                    pe.wait_ge(v_done, 4 * LAYERS)
                else:
                    need(pe, p_done, 2 * k)
                pe.wait_ge(qhi_done, 2 * k + h + 1)
                for n in range(NB):
                    mm = pe.matmul(mx_ps[h][:, n * T:(n + 1) * T], qe[:, i % 2, h, n * P:(n + 1) * P],
                                   km[:, 2 * i + h, :], start=True, stop=True)
                mm.then_inc(mx_done, 1)

            def turn_maxima(k, c, i):
                pe.wait_ge(mred_done, 2 * k + 2)
                pe.transpose(mx_ps[0][:, 0:P], mneg[:, i % 2, :, :].rearrange("p n c -> p (n c)"), ident[:, :])\
                  .then_inc(mt_done, 1)

            def probs_v(k, c, i):
                if i % 4 == 0:
                    pe.wait_ge(v_in[i // 4], 16 * (c + 1))
                if isinstance(k, int) and k == PAIRS * TOTAL - 1:
                    pe.wait_ge(p_done, 2 * k + 2)
                need(pe, oun_done, k)
                for h in range(2):
                    hd = 2 * i + h
                    mm = pe.matmul(pv_ps[h * D:(h + 1) * D, :], v[:, hd * D:(hd + 1) * D], probs[:, i % 2, h, :],
                                   start=True, stop=True)
                mm.then_inc(pv_done, 1)

            def denominators(k, c, i):
                pe.wait_ge(fold_done, 2 * k + 2)
                need(pe, rec_raw, 2 * c + i // 4)
                for j in range(4):
                    mm = pe.matmul(sum_ps[32 * j:32 * j + 32, :], ssel[:, :], fold[:, j, :], start=True, stop=True)
                mm.then_inc(sum_done, 1)

            def project_q(k, c, i, products):
                if products[0] == 0:
                    if i == 0:
                        pe.wait_ge(x_hi_done, XT * (c + 1))
                    if isinstance(c, int) and c == NCH:
                        pe.wait_ge(sl_lo[0], i + 1)
                    need(pe, qhi_done, 2 * k)
                    need(pe, qlo_done, 2 * k)
                for n in products:
                    wt, xx = ((wq_hi, x_hi), (wq_lo, x_hi), (wq_hi, x_lo))[n // XT]
                    t = n % XT
                    if i == 0 and n == 2 * XT:
                        pe.wait_ge(x_lo_done, XT * (c + 1))
                    mm = pe.matmul(q_ps[:, :], wt[:, i, t, :], xx[:, t, :], start=(n == 0), stop=(n == 3 * XT - 1))
                if products[-1] == 3 * XT - 1:
                    mm.then_inc(q_done, 1)

            def project_out(k, c, i, lc):
                hf, t = i // 4, i % 4
                if lc or isinstance(c, int) and c == 0:
                    pe.wait_ge(sl_lo[1], lc * PAIRS + i + 1)
                if final(c):
                    need(pe, res_done, k - 4 if i >= 5 else PAIRS * c)
                else:
                    need(pe, res_done, k)
                for kk in range(4):
                    if t == 0:
                        pe.wait_ge(o_done, PAIRS * c + 4 * hf + kk + 1)
                    for n, (wt, oo) in enumerate(((wo_hi, o_hi), (wo_lo, o_hi), (wo_hi, o_lo))):
                        mm = pe.matmul(out_bank(c, i)[:, :], wt[:, hf, t, kk, :], oo[:, 4 * hf + kk, :],
                                       start=(kk == 0 and n == 0), stop=(kk == 3 and n == 2))
                mm.then_inc(out_done, 1)

            def step(g, s, layer):
                now, ahead, far = pair(g, s, 0), pair(g, s, 1), pair(g, s, AHEAD)
                last, norm, unit = pair(g, s, -1), pair(g, s, -NORM), pair(g, s, -PAIRS)
                if norm and s % 4 == 0 and not (final(norm[1]) and norm[2] == PAIRS - 1):
                    spread(*norm)
                if now:
                    logits(*now)
                if last:
                    probs_v(*last)
                    if last[2] % 4 == 3:
                        denominators(*last)
                if ahead:
                    maxima(*ahead, 0)
                late = isinstance(g, int) and g == TOTAL and 0 < s < 4
                if unit and ahead and not far:
                    maxima(*ahead, 1)
                    turn_maxima(*ahead)
                    ahead = None
                if norm and s % 4 and not late:
                    spread(*norm)
                if ahead:
                    maxima(*ahead, 1)
                if unit:
                    project_out(*unit, layer_of(unit[1], layer))
                if late:
                    for off in (0, 1) if s == 1 else (1,):
                        spread(*pair(g, s, off - NORM))
                if far:
                    start = 0 if unit or not ahead else 6
                    if start:
                        project_q(*far, range(start))
                    if ahead:
                        turn_maxima(*ahead)
                    project_q(*far, range(start, 3 * XT))
                elif ahead:
                    turn_maxima(*ahead)

            chunks(pe, step)

        @block.scalar
        def _(act):
            act.dma_start(m_f, masks.rearrange("a (r n) -> (a r) n", n=P)).then_inc(small_in, 16)
            act.dma_start(ints[:, 0:2 * LAYERS * NI], idx.partition_broadcast(P)).then_inc(small_in, 16)
            act.dma_start(bo_s[:, :, :], bo.rearrange("p (l t) -> p l t", t=XT)).then_inc(small_in, 16)

            def split_x(c):
                act.wait_ge(x_in, 16 * (c + 1))
                need(act, q_done, PAIRS * c)
                for t in range(XT):
                    nc.scalar.copy(x_hi[:, t, :], x_f[:, t, :]).then_inc(x_hi_done, 1)

            for n, (l, w) in enumerate(TILES):
                sl = n % 4
                if n < 4:
                    act.wait_ge(c_in[n], 16)
                    nc.scalar.copy(c_hi[:, 2 * n:2 * n + 2, :], c_f[:, 2 * n:2 * n + 2, :]).then_inc(c_hi_done, 1)
                act.wait_ge(w_in[sl], 16 * (n // 4 + 1))
                if l is not None:
                    need(act, w_used, l * W_TILES + w - 3)
                    nc.scalar.copy(s_hi[w % 4], stage[sl]).then_inc(w_hi_done, 1)
                else:
                    nc.scalar.copy(wq_hi[:, :, w, :], stage[sl].rearrange("p (m c) -> p m c", c=P)).then_inc(w_hi_done, 1)
                if l == 1 and w == 2:
                    split_x(0)
                if l is not None and w == KTL + 1:
                    act.wait_ge(w_used, l * W_TILES + KTL)
                    if l:
                        act.wait_ge(k_out, 16 * K_STORES * l)
                    for m in range(4):
                        nc.scalar.mul(k_hi[:, m * 512:(m + 1) * 512], banks[m][:, :], SCALE).then_inc(k_hi_done, 1)
                if (l, w) == (1, 1) or n == len(TILES) - 1:
                    lv = int(w != 1)
                    act.wait_ge(w_used, (lv + 1) * W_TILES)
                    if lv:
                        act.wait_ge(v_out, 16 * lv)
                    for m in range(4):
                        nc.scalar.copy(v_s[:, m // 2, (m % 2) * 512:(m % 2 + 1) * 512], banks[4 + m][:, :]).then_inc(v_done, 1)
                    act.wait_ge(v_done, 4 * (lv + 1))
                    act.dma_start(v_d[lv * B:(lv + 1) * B, :, :].rearrange("b t n -> t b n"), v_s).then_inc(v_out, 16)
            act.wait_ge(k_out, 16 * K_STORES * LAYERS)
            act.wait_ge(w_lo_done, len(TILES))

            def q_hi(k, c, i):
                act.wait_ge(q_done, k + 1)
                for h in range(2):
                    need(act, lg_done, 2 * k + h - 3)
                    nc.scalar.copy(qe[0:D, i % 2, h, :], q_ps[h * D:(h + 1) * D, :]).then_inc(qhi_done, 1)

            def exps(k, c, i):
                if isinstance(k, int) and k == 0:
                    act.wait_ge(v_out, 16 * LAYERS)
                need(act, pv_done, k - 1)
                need(act, fold_done, 2 * k - 2)
                for h in range(2):
                    act.wait_ge(lg_done, 2 * k + h + 1)
                    nc.scalar.activation(probs[:, i % 2, h, :], lg_ps[h][:, :], ACT.Exp).then_inc(p_done, 1)

            def halves(k, c, i):
                if i % 4 == 0:
                    need(act, sum_done, 2 * c + i // 4)
                for h in range(2):
                    act.wait_ge(p_done, 2 * k + h + 1)
                    nc.scalar.copy(fold[h * D:(h + 1) * D, i % 4, :], probs[(1 - h) * D:(2 - h) * D, i % 2, h, :])\
                      .then_inc(half_done, 1)

            def q_dup(k, c, i):
                act.wait_ge(qhi_done, 2 * k + 2)
                nc.scalar.copy(qt[0:D, i % 2, :, :], qe[0:D, i % 2, :, :]).then_inc(qdup_done, 1)

            def copy_o(k, c, i):
                act.wait_ge(pv_done, k + 1)
                need(act, o_done, k - 3)
                nc.scalar.copy(o_f[:, i % 4, :], pv_ps[:, :]).then_inc(oun_done, 1)

            def max_rows(k, c, i):
                act.wait_ge(mt_done, k + 1)
                for n in range(NB):
                    nc.scalar.copy(qe[MRW:P, i % 2, :, n * P:(n + 1) * P],
                                   mx_ps[0][32 * n:32 * n + 32, 0:P].unsqueeze(1).to_broadcast([32, 2, P])).then_inc(mrow_done, 1)

            def slice_hi(which, n, slot, dst, s_used, used):
                act.wait_ge(sl_in[which][slot], 16 * (n // 2 + 1))
                act.wait_ge(s_used, used)
                nc.scalar.copy(dst, w_st[:, slot, :, :]).then_inc(sl_hi[which], 1)

            def step(g, s, layer):
                now, ahead, last = pair(g, s, 0), pair(g, s, 1), pair(g, s, -1)
                if ahead:
                    q_hi(*ahead)
                if now:
                    exps(*now)
                if s == 6 and (not isinstance(g, int) or 0 <= g < TOTAL - 1):
                    split_x(g + 1)
                if now:
                    halves(*now)
                if ahead:
                    q_dup(*ahead)
                if ahead:
                    max_rows(*ahead)
                if last:
                    copy_o(*last)
                if isinstance(g, int) and g == NCH - 1:
                    slice_hi(0, s, s % 2, wq_hi[:, s, :, :], q_done, PAIRS * g + s + 1)
                if isinstance(g, int) and g == 0:
                    slice_hi(1, s, s % 2, wo_hi[:, s // 4, s % 4, :, :], w_used, KV)
                if isinstance(g, int) and g == NCH:
                    for n in ([s - 1] if s else []) + ([s] if s == PAIRS - 1 else []):
                        slice_hi(1, PAIRS + n, n % 2, wo_hi[:, n // 4, n % 4, :, :], out_done, PAIRS * (g - 1) + n + 1)

            chunks(act, step)

        @block.vector
        def _(dve):
            chain = [0]

            def link(ins):
                chain[0] += 1
                ins.then_inc(consts, 1)
                dve.wait_ge(consts, chain[0])

            def bias_rows():
                rows = m_f
                link(nc.vector.tensor_scalar(rows, rows, -1.0, 1.0, ALU.mult, ALU.add))
                link(nc.vector.tensor_scalar(rows, rows, -SUPPRESS / 2, None, ALU.mult))
                link(nc.vector.tensor_copy(m_hi, rows))
                link(nc.vector.tensor_tensor(m_lo, rows, m_hi, ALU.subtract))

            row_m = row_s[:, 13:14]

            def is_row(dst, lo, hi, row=row_s[:, 0:1]):
                link(nc.vector.tensor_scalar(dst, row, float(lo), None, ALU.is_ge))
                link(nc.vector.scalar_tensor_tensor(out=dst, in0=row, scalar=float(hi), in1=dst,
                                                    op0=ALU.is_lt, op1=ALU.mult))

            def tables():
                dve.wait_ge(pool_c, 2)
                link(nc.vector.tensor_copy(tok[:, 0:T], ints[:, 64:64 + T]))
                link(nc.vector.tensor_copy(row_s[:, 0:1], ints[:, 32:33]))
                link(nc.vector.tensor_scalar(ident[:, :], tok[:, 0:P], row_s[:, 0:1], None, ALU.is_equal))

                for n, lo in enumerate((SUP, SUP + 2)):
                    is_row(row_s[:, 1 + n:2 + n], lo, lo + 2)
                for h in range(2):
                    is_row(row_s[:, 3 + h:4 + h], MRW + h, MRW + h + 1)
                link(nc.vector.tensor_scalar(row_m, row_s[:, 0:1], float(D), None, ALU.is_ge))
                link(nc.vector.scalar_tensor_tensor(out=row_m, in0=row_m, scalar=float(-D), in1=row_s[:, 0:1],
                                                    op0=ALU.mult, op1=ALU.add))

            def selector(n):
                for h in range(2):
                    c0 = 5 + 2 * n + h
                    is_row(row_s[:, c0:c0 + 1], 32 * n + h, 32 * n + h + 1, row_m)
                    link(nc.vector.tensor_scalar(rsel[:, n, h * D:(h + 1) * D], tok[:, 0:D], 0.0,
                                                 row_s[:, c0:c0 + 1], ALU.mult, ALU.add))

            def token_set(l, a, dst):
                at = (2 * l + a) * NI
                link(nc.vector.tensor_scalar(dst, tok[:, 0:T], idx_f[:, at:at + 1], None, ALU.is_equal))
                for n in range(at + 1, at + NI):
                    link(nc.vector.scalar_tensor_tensor(out=dst, in0=tok[:, 0:T], scalar=idx_f[:, n:n + 1],
                                                        in1=dst, op0=ALU.is_equal, op1=ALU.max))

            def indicators(l):
                link(nc.vector.tensor_scalar(ind_n, ind_b, -1.0, 1.0, ALU.mult, ALU.add))
                link(nc.vector.tensor_tensor(ind_a, ind_a, ind_n, ALU.mult))
                for h in range(2):
                    link(nc.vector.tensor_scalar(ind_n, ind_a, row_s[:, 1:2], row_s[:, 3 + h:4 + h], ALU.mult, ALU.add))
                    link(nc.vector.scalar_tensor_tensor(out=ext[:, l, h, :], in0=ind_b, scalar=row_s[:, 2:3], in1=ind_n,
                                                        op0=ALU.mult, op1=ALU.add))

            def split_x(c):
                for t in range(XT):
                    dve.wait_ge(x_hi_done, XT * c + t + 1)
                    nc.vector.tensor_tensor(x_lo[:, t, :], x_f[:, t, :], x_hi[:, t, :], ALU.subtract).then_inc(x_lo_done, 1)

            tables()
            for n, (l, w) in enumerate(TILES):
                sl = n % 4
                if n < 4:
                    dve.wait_ge(c_hi_done, n + 1)
                    ks = slice(2 * n, 2 * n + 2)
                    nc.vector.tensor_tensor(c_lo[:, ks, :], c_f[:, ks, :], c_hi[:, ks, :], ALU.subtract).then_inc(c_lo_done, 1)
                dve.wait_ge(w_hi_done, n + 1)
                if l is not None:
                    nc.vector.tensor_tensor(s_lo[w % 4], stage[sl], s_hi[w % 4], ALU.subtract).then_inc(w_lo_done, 1)
                else:
                    nc.vector.tensor_tensor(wq_lo[:, :, w, :], stage[sl].rearrange("p (m c) -> p m c", c=P), wq_hi[:, :, w, :],
                                            ALU.subtract).then_inc(w_lo_done, 1)
                if n == 4:
                    dve.wait_ge(small_in, 16 * 3)
                    link(nc.vector.tensor_copy(idx_f, ints[:, 0:2 * LAYERS * NI]))
                    link(nc.vector.tensor_scalar(idx_w, idx_f, 0.0, float(T), ALU.is_lt, ALU.mult))
                    link(nc.vector.tensor_tensor(idx_f, idx_f, idx_w, ALU.add))
                    bias_rows()
                if l == 0 and 5 <= w < 7:
                    selector(w - 5)
                if l == 0 and w in (10, 12):
                    for a, dst in enumerate((ind_a, ind_b)):
                        token_set((w - 10) // 2, a, dst)
                if l == 0 and w in (11, 13):
                    indicators((w - 11) // 2)
                if l == 1 and w == 2:
                    split_x(0)
                if l is not None and w == KTL + 1:
                    for m in range(4):
                        dve.wait_ge(k_hi_done, 4 * l + m + 1)
                        ms = slice(m * 512, (m + 1) * 512)
                        nc.vector.scalar_tensor_tensor(out=k_lo[:, ms], in0=banks[m][:, :], scalar=SCALE, in1=k_hi[:, ms],
                                                       op0=ALU.mult, op1=ALU.subtract).then_inc(k_lo_done, 1)
            assert chain[0] == DVE_CONSTS, chain[0]
            dve.wait_ge(k_out, 16 * K_STORES * LAYERS)

            def q_lo(k, c, i):
                for h in range(2):
                    dve.wait_ge(qhi_done, 2 * k + h + 1)
                    need(dve, lg_done, 2 * k + h - 3)
                    nc.vector.tensor_tensor(qt[D:P, i % 2, h, :], q_ps[h * D:(h + 1) * D, :], qe[0:D, i % 2, h, :],
                                            ALU.subtract).then_inc(qlo_done, 1)

            def row_max(k, c, i, h):
                dve.wait_ge(mx_done, 2 * k + h + 1)
                if h == 0:
                    need(dve, mt_done, k - 1)
                nc.vector.tensor_reduce(mneg[:, i % 2, :, h], mx_ps[h][:, :].rearrange("p (n t) -> p n t", t=T), AX_X,
                                        ALU.max, negate=True).then_inc(mred_done, 1)

            def normalise(k, c, i):
                dve.wait_ge(bc_done, k + 1)
                dve.wait_ge(oun_done, k + 1)
                nc.vector.tensor_tensor(o_f[:, i % 4, :], o_f[:, i % 4, :], bc_bank(c, i)[:, :], ALU.mult).then_inc(on_done, 1)

            def split_o(k, c, i):
                need(dve, out_done, PAIRS * c + 4 * (i // 4) - 4)
                dve.wait_ge(on_done, k + 1)
                nc.vector.tensor_copy(o_hi[:, i, :], o_f[:, i % 4, :]).then_inc(oh_done, 1)
                dve.wait_ge(oh_done, k + 1)
                nc.vector.tensor_tensor(o_lo[:, i, :], o_f[:, i % 4, :], o_hi[:, i, :], ALU.subtract).then_inc(o_done, 1)

            def reciprocals(k, c, i):
                n = 2 * c + i // 4
                dve.wait_ge(sum_done, n + 1)
                nc.vector.reciprocal(rec[:, :], sum_ps[:, :]).then_inc(rec_raw, 1)
                need(dve, bc_done, 4 * n)
                dve.wait_ge(rec_raw, n + 1)
                for a in range(2):
                    nc.vector.tensor_copy(rec_s[0:D, a, :], rec[a * D:(a + 1) * D, :]).then_inc(rec_h, 1)
                    dve.wait_ge(rec_h, 2 * n + a + 1)
                    nc.vector.tensor_tensor(rec_s[D:P, a, :], rec[a * D:(a + 1) * D, :], rec_s[0:D, a, :],
                                            ALU.subtract).then_inc(rec_done, 1)

            def add_out(k, c, i, lc):
                hf, t = i // 4, i % 4
                bank = out_bank(c, i)
                dve.wait_ge(out_done, k + 1)
                if hf == 0:
                    dve.wait_ge(r_in[t], 16 * (c + 1))
                    ins = nc.vector.scalar_tensor_tensor(out=res[:, t, :], in0=bank[:, :], scalar=bo_s[:, lc, t:t + 1],
                                                         in1=res[:, t, :], op0=ALU.add, op1=ALU.add)
                else:
                    dve.wait_ge(res_done, k - 3)
                    ins = nc.vector.tensor_tensor(res[:, t, :], bank[:, :], res[:, t, :], ALU.add)
                ins.then_inc(res_done, 1)

            def slice_lo(which, n, slot, dst, hi):
                dve.wait_ge(sl_hi[which], n + 1)
                nc.vector.tensor_tensor(dst, w_st[:, slot, :, :], hi, ALU.subtract).then_inc(sl_lo[which], 1)

            def step(g, s, layer):
                ahead, last, norm, unit = pair(g, s, 1), pair(g, s, -1), pair(g, s, -NORM), pair(g, s, -PAIRS)
                if norm and s % 4 == 0:
                    normalise(*norm)
                if ahead:
                    q_lo(*ahead)
                if norm and s % 4 == 0:
                    split_o(*norm)
                if ahead:
                    row_max(*ahead, 0)
                    row_max(*ahead, 1)
                if s == 6 and (not isinstance(g, int) or 0 <= g < TOTAL - 1):
                    split_x(g + 1)
                if norm and s % 4:
                    normalise(*norm)
                    split_o(*norm)
                if last and last[2] % 4 == 3:
                    reciprocals(*last)
                if unit and final(unit[1]):
                    for i in range(5) if s == 4 else [s] if s > 4 else []:
                        add_out(PAIRS * unit[1] + i, unit[1], i, LAYERS - 1)
                elif unit:
                    add_out(*unit, layer_of(unit[1], layer))
                if isinstance(g, int) and g == NCH - 1:
                    slice_lo(0, s, s % 2, wq_lo[:, s, :, :], wq_hi[:, s, :, :])
                if isinstance(g, int) and g == 0:
                    slice_lo(1, s, s % 2, wo_lo[:, s // 4, s % 4, :, :], wo_hi[:, s // 4, s % 4, :, :])
                if isinstance(g, int) and g == NCH:
                    for n in ([s - 1] if s else []) + ([s] if s == PAIRS - 1 else []):
                        slice_lo(1, PAIRS + n, n % 2, wo_lo[:, n // 4, n % 4, :, :], wo_hi[:, n // 4, n % 4, :, :])

            chunks(dve, step)

        @block.gpsimd
        def _(pool):
            nc.gpsimd.iota(ints[:, 64:64 + T], pattern=[[1, T]], base=0, channel_multiplier=0).then_inc(pool_c, 1)
            nc.gpsimd.iota(ints[:, 32:33], pattern=[[0, 1]], base=0, channel_multiplier=1).then_inc(pool_c, 1)
            nc.gpsimd.memset(mneg[:, :, :, :], 0.0).then_inc(pool_c, 1)
            nc.gpsimd.memset(ssel[:, :], 1.0).then_inc(pool_c, 1)
            pool.wait_ge(pool_c, 4)
            nc.gpsimd.memset(ssel[D:P, 0:1], 0.0).then_inc(pool_c, 1)
            pool.wait_ge(pool_c, 5)
            nc.gpsimd.memset(ssel[0:D, 1:2], 0.0).then_inc(pool_c, 1)
            pool.wait_ge(consts, DVE_CONSTS)
            for l in range(LAYERS):
                pool.dma_start(ext_d[l, :, :], ext[SUP:P, l, :, :].bitcast(F32).rearrange("p a t -> p (a t)")).then_inc(ext_out, 16)
            pool.wait_ge(ext_out, 16 * LAYERS)
            pool.wait_ge(pool_c, POOL_CONSTS - 1)
            nc.gpsimd.memset(sup_c[SUP:P, :].bitcast(F32), 0.0).then_inc(pool_c, 1)
            pool.wait_ge(pool_c, POOL_CONSTS)
            pool.wait_ge(k_out, 16 * K_STORES * LAYERS)

            def rows(k, c, i):
                need(pool, lg_done, 2 * k - 2)
                need(pool, fold_done, 2 * k - 4)
                if i == 0:
                    pool.wait_ge(sup_in, 16 * (c + 1))
                for h in range(2):
                    src = sup_c[SUP:P, :].bitcast(F32)
                    nc.gpsimd.tensor_tensor(qe[SUP:P, i % 2, h, :], src, src, ALU.add).then_inc(mz_done, 1)

            def folds(k, c, i):
                pool.wait_ge(mz_done, min(2 * k + 6, 2 * PAIRS * TOTAL) if isinstance(k, int) else 2 * k + 6)
                for h in range(2):
                    at = slice(h * D, (h + 1) * D)
                    pool.wait_ge(half_done, 2 * k + h + 1)
                    if h:
                        pool.wait_ge(fold_done, 2 * k + 1)
                    nc.gpsimd.tensor_tensor(fold[at, i % 4, :], fold[at, i % 4, :], probs[at, i % 2, h, :],
                                            ALU.add).then_inc(fold_done, 1)

            def step(g, s, layer):
                now, far = pair(g, s, 0), pair(g, s, AHEAD)
                if far:
                    rows(*far)
                if now:
                    folds(*now)

            chunks(pool, step)


def kernel(**inputs):
    import numpy as np
    import concourse.bacc as bacc
    from concourse.bass_utils import run_bass_kernel_spmd

    a = {k: np.asarray(x) for k, x in inputs.items()}
    Bn, HWn, Cn = a["x"].shape
    lay = ("L0_xattn_", "L1_xattn_")
    arrays = {
        "xT": np.ascontiguousarray(a["x"].reshape(Bn * HWn, Cn).T),
        "ctxT": np.ascontiguousarray(a["ctx_2048"].reshape(-1, a["ctx_2048"].shape[-1]).T),
        "masks": np.stack([a["mask_S_fk1"], a["mask_S_fk0"]]),
        "Wk": np.stack([a[l + "Wk"] for l in lay]),
        "Wv": np.stack([a[l + "Wv"] for l in lay]),
        "Wq": np.stack([a[l + "Wq"] for l in lay]),
        "Wo": np.stack([a[l + "Wo"] for l in lay]),
        "bo": np.ascontiguousarray(np.stack([a[l + "bo"] for l in lay]).reshape(-1, P).T),
        "idx": np.concatenate([a[l + "token_indices_" + s] for l in lay for s in "AB"])[None, :],
    }
    nc = bacc.Bacc("TRN2", target_bir_lowering=False, num_devices=1)
    args = [nc.dram_tensor(n, x.shape, mybir.dt.from_np(x.dtype), kind="ExternalInput").ap() for n, x in arrays.items()]
    yT = nc.dram_tensor("yT", (Cn, Bn * HWn), F32, kind="ExternalOutput").ap()
    two_cross_attentions(nc, *args, yT)
    r = run_bass_kernel_spmd(nc, [arrays], core_ids=[0])
    return np.ascontiguousarray(r.results[0]["yT"].T).reshape(Bn, HWn, Cn)
```

```python
from contextlib import ExitStack

import concourse.bass as bass
from concourse import mybir

F32 = mybir.dt.float32
F32R = mybir.dt.float32r
I32 = mybir.dt.int32
ALU = mybir.AluOpType
ACT = mybir.ActivationFunctionType
AX_X = mybir.AxisListType.X

P = 128
LAYERS = 2
SUPPRESS = 20.0


def two_cross_attentions(nc, xT, ctxT, masks, Wk, Wv, Wq, Wo, bo, idx, yT):
    C, ROWS = xT.shape
    CT, BT = ctxT.shape
    HW = masks.shape[1]
    INNER = Wk.shape[2]
    B = ROWS // HW
    T = BT // B
    NI = idx.shape[1] // (2 * LAYERS)
    D = 64
    H = INNER // D
    PAIRS = H // 2
    Q = 512
    NCH = ROWS // Q
    CPB = HW // Q
    TOTAL = LAYERS * NCH
    XT = C // P
    KTL = CT // P
    NB = Q // P
    SCALE = float(D) ** -0.5
    SUP = 64
    MRW = 96
    AHEAD = 2
    NORM = 5
    assert T == P and PAIRS == 8 and XT == 4 and NB == 4 and NCH == 8 and B == 2

    kh_d = nc.dram_tensor("kh_d", (LAYERS * B, P, PAIRS * T), F32, kind="Internal").ap()
    kl_d = nc.dram_tensor("kl_d", (LAYERS * B, P, PAIRS * T), F32, kind="Internal").ap()
    ext_d = nc.dram_tensor("ext_d", (LAYERS, P - SUP, 2 * T), F32, kind="Internal").ap()
    v_d = nc.dram_tensor("v_d", (LAYERS * B, T, INNER), F32, kind="Internal").ap()
    sup_d = nc.dram_tensor("sup_d", (4, HW), F32, kind="Internal").ap()
    rec_d = nc.dram_tensor("rec_d", (2, 2, 4, Q), F32, kind="Internal").ap()
    x1_d = nc.dram_tensor("x1_d", (C, ROWS), F32, kind="Internal").ap()

    with ExitStack() as ctx:
        def sb(name, shape, dt):
            return ctx.enter_context(nc.sbuf_tensor(name, shape, dt))

        def sem(name):
            return ctx.enter_context(nc.semaphore(name))

        wq_hi = sb("wq_hi", [P, PAIRS, XT, P], F32R)
        wq_lo = sb("wq_lo", [P, PAIRS, XT, P], F32R)
        wo_hi = sb("wo_hi", [P, 2, XT, 4, P], F32R)
        wo_lo = sb("wo_lo", [P, 2, XT, 4, P], F32R)
        km = sb("km", [P, H, T], F32R)
        kt = sb("kt", [P, H, T], F32R)
        v = sb("v", [P, INNER], F32)
        x_f = sb("x_f", [P, XT, Q], F32)
        x_hi = sb("x_hi", [P, XT, Q], F32R)
        x_lo = sb("x_lo", [P, XT, Q], F32R)
        qe = sb("qe", [P, 2, 2, Q], F32R)
        qt = sb("qt", [P, 2, 2, Q], F32R)
        probs = sb("probs", [P, 2, 2, Q], F32)
        fold = sb("fold", [P, 4, Q], F32)
        o_f = sb("o_f", [P, 4, Q], F32)
        o_hi = sb("o_hi", [P, 8, Q], F32R)
        o_lo = sb("o_lo", [P, 8, Q], F32R)
        res = sb("res", [P, XT, Q], F32)
        w_st = sb("w_st", [P, 2, 4, P], F32)
        rec = sb("rec", [P, Q], F32)
        bc = sb("bc", [P, 2, Q], F32)
        sup_c = sb("sup_c", [P, Q], F32R)
        mneg = sb("mneg", [P, 2, NB, 32], F32)
        ident = sb("ident", [P, P], F32)
        warm = sb("warm", [P, 1], F32)
        m_s = sb("m_s", [P, 2, P], F32R)
        ssel = sb("ssel", [P, 32], F32)
        bo_s = sb("bo_s", [P, LAYERS, XT], F32)

        c_f = x_f[:, :, :].rearrange("p a (b n) -> p (a b) n", n=BT)
        c_hi = wo_hi[:, 0, :, :, :].rearrange("p a b n -> p (a b n)").rearrange("p (k n) -> p k n", n=BT)
        c_lo = wo_lo[:, 0, :, :, :].rearrange("p a b n -> p (a b n)").rearrange("p (k n) -> p k n", n=BT)
        stage = [res[:, 0:2, :], res[:, 2:4, :], o_f[:, 0:2, :], o_f[:, 2:4, :]]
        stage = [s.rearrange("p a b -> p (a b)") for s in stage]
        s_hi = [o_hi[:, 2 * i:2 * i + 2, :].rearrange("p a b -> p (a b)") for i in range(4)]
        s_lo = [o_lo[:, 2 * i:2 * i + 2, :].rearrange("p a b -> p (a b)") for i in range(4)]
        k_hi = qt[:, :, :, :].rearrange("p a b n -> p (a b n)")
        k_lo = qe[:, :, :, :].rearrange("p a b n -> p (a b n)")
        v_s = [bc[:, :, :], fold[:, 2:4, :]]
        tok = rec
        ind = fold[:, 0:2, :].rearrange("p a n -> p (a n)")
        ind_a, ind_b, ind_n = (ind[:, i * T:(i + 1) * T] for i in range(3))
        idx_f = ind[:, 3 * T:3 * T + 2 * LAYERS * NI]
        idx_w = ind[:, 3 * T + 32:3 * T + 32 + 2 * LAYERS * NI]
        row_s = ind[:, 3 * T + 64:3 * T + 128]
        ints = fold[:, 2, :].bitcast(I32)
        ext = sup_c[:, :].rearrange("p (l a t) -> p l a t", l=LAYERS, a=2)
        MR = 2 * HW // P
        m_f, m_hi, m_lo = w_st[0:MR, 0, 0, :], m_s[0:MR, 0, :], m_s[0:MR, 1, :]

        banks = [ctx.enter_context(nc.psum_tensor(f"bank{i}", [P, 512], F32)) for i in range(8)]
        q_ps, out_ps = banks[0], banks[3]
        lg_ps = [banks[4], banks[5]]
        mx_ps = [banks[1], banks[2]]
        pv_ps, sum_ps = banks[6], banks[7]

        c_in = [sem(f"c_in{i}") for i in range(4)]
        c_hi_done = sem("c_hi_done")
        c_lo_done = sem("c_lo_done")
        w_in = [sem(f"w_in{i}") for i in range(4)]
        w_hi_done = sem("w_hi_done")
        w_lo_done = sem("w_lo_done")
        w_used = sem("w_used")
        k_hi_done = sem("k_hi_done")
        k_lo_done = sem("k_lo_done")
        k_out = sem("k_out")
        v_done = sem("v_done")
        v_out = sem("v_out")
        consts = sem("consts")
        pool_c = sem("pool_c")
        small_in = sem("small_in")
        sup_out = sem("sup_out")
        ext_out = sem("ext_out")
        x_in = sem("x_in")
        x_hi_done = sem("x_hi_done")
        x_lo_done = sem("x_lo_done")
        sup_in = sem("sup_in")
        km_in = [sem(f"km_in{i}") for i in range(2)]
        kt_in = [sem(f"kt_in{i}") for i in range(2)]
        v_in = [sem(f"v_in{i}") for i in range(2)]
        q_done = sem("q_done")
        qhi_done = sem("qhi_done")
        qlo_done = sem("qlo_done")
        qdup_done = sem("qdup_done")
        mz_done = sem("mz_done")
        mx_done = sem("mx_done")
        mred_done = sem("mred_done")
        mt_done = sem("mt_done")
        mrow_done = sem("mrow_done")
        lg_done = sem("lg_done")
        p_done = sem("p_done")
        pv_done = sem("pv_done")
        half_done = sem("half_done")
        fold_done = sem("fold_done")
        sum_done = sem("sum_done")
        oun_done = sem("oun_done")
        rec_raw = sem("rec_raw")
        rec_out = sem("rec_out")
        bc_in = [sem(f"bc_in{i}") for i in range(2)]
        on_done = sem("on_done")
        oh_done = sem("oh_done")
        o_done = sem("o_done")
        out_done = sem("out_done")
        res_done = sem("res_done")
        r_in = [sem(f"r_in{i}") for i in range(XT)]
        y_out = [sem(f"y_out{i}") for i in range(XT)]
        sl_in = [[sem(f"{w}_sl_in{i}") for i in range(2)] for w in ("wq", "wo")]
        sl_hi = [sem("wq_sl_hi"), sem("wo_sl_hi")]
        sl_lo = [sem("wq_sl_lo"), sem("wo_sl_lo")]

        block = ctx.enter_context(nc.Block())

        W_TILES = 2 * KTL
        KV = LAYERS * W_TILES
        K_STORES = 2 * B
        TILES = []
        for n in range(KV):
            TILES.append((n // W_TILES, n % W_TILES))
            if n % 8 == 5:
                TILES.append((None, n // 8))
        BIAS_STEPS = 3 + 8 + 3 + 4
        DVE_CONSTS = BIAS_STEPS + LAYERS * (2 * NI + 2 + 4)
        POOL_CONSTS = 7

        def need(eng, s, count):
            if not isinstance(count, int) or count > 0:
                eng.wait_ge(s, count)

        def pair(g, s, off):
            i = s + off
            dg, i = i // PAIRS, i % PAIRS
            c = g + dg
            if isinstance(c, int) and not 0 <= c < TOTAL:
                return None
            return c * PAIRS + i, c, i

        def chunks(eng, step):
            for s in (6, 7):
                step(-1, s, 0)
            for layer in range(LAYERS):
                g0 = layer * NCH
                alone = range(2) if layer == 0 else range(g0, g0 + 1)
                for g in alone:
                    for s in range(PAIRS):
                        step(g, s, layer)
                with eng.Fori(alone[-1] + 1, g0 + NCH - 1) as g:
                    for s in range(PAIRS):
                        step(g, s, layer)
                for s in range(PAIRS):
                    step(g0 + NCH - 1, s, layer)
            for s in range(PAIRS):
                step(TOTAL, s, LAYERS - 1)

        def final(c):
            return isinstance(c, int) and c == TOTAL - 1

        def out_bank(c, i):
            return (out_ps, q_ps, mx_ps[0], lg_ps[0], lg_ps[1])[i % 5] if final(c) else out_ps

        def layer_of(g, layer):
            return g // NCH if isinstance(g, int) else layer

        @block.sync
        def _(sp):
            def w_load(n):
                need(sp, w_lo_done, n - 3)
                l, w = TILES[n]
                kk = w % KTL
                src = Wq[0, w * P:(w + 1) * P, :] if l is None else (Wk if w < KTL else Wv)[l, kk * P:(kk + 1) * P, :]
                sp.dma_start(stage[n % 4], src).then_inc(w_in[n % 4], 16)

            for i in range(4):
                ks = slice(2 * i, 2 * i + 2)
                sp.dma_start(c_f[:, ks, :], ctxT[2 * i * P:(2 * i + 2) * P, :].rearrange("(k p) n -> p k n", p=P))\
                  .then_inc(c_in[i], 16)
                w_load(i)

            def index(value):
                return value if isinstance(value, int) else sp.snap(value)

            def load_x(c, layer):
                need(sp, x_lo_done, XT * c)
                src = xT if layer == 0 else x1_d
                if layer:
                    for t in range(XT):
                        sp.wait_ge(y_out[t], 16 * (c - NCH + 1))
                col = (c - layer * NCH) * Q
                sp.dma_start(x_f[:, :, :], src[:, bass.ds(col, Q)].rearrange("(t p) n -> p t n", p=P)).then_inc(x_in, 16)

            def load_sup(c):
                at = index(c % CPB)
                need(sp, mz_done, 2 * PAIRS * c)
                sp.dma_start(sup_c[SUP:SUP + 4, :].bitcast(F32), sup_d[:, bass.ds(at * Q, Q)]).then_inc(sup_in, 16)

            def load_k(c, half, layer):
                lb = index(c // CPB)
                need(sp, lg_done, 2 * (PAIRS * (c - 1) + 4 * (half + 1)))
                heads = slice(half * 8, half * 8 + 8)
                ms = slice(half * 4 * T, (half + 1) * 4 * T)
                end = P if isinstance(c, int) and c == 0 else SUP + 4
                sp.dma_start(km[SUP:end, heads, :].rearrange("p (m h) t -> p m (h t)", h=2).bitcast(F32),
                             ext_d[layer, 0:end - SUP, :].unsqueeze(1).to_broadcast([end - SUP, PAIRS // 2, 2 * T]))\
                  .then_inc(km_in[half], 16)
                for dst, k_d, done in ((km[0:D, heads, :], kh_d, km_in), (kt[0:D, heads, :], kl_d, kt_in),
                                       (kt[D:P, heads, :], kh_d, kt_in)):
                    dst = dst.rearrange("d (m h) t -> d h m t", h=2).bitcast(F32)
                    for h in range(2):
                        sp.dma_start(dst[:, h, :, :], k_d[lb, h * D:(h + 1) * D, ms].rearrange("d (m t) -> d m t", t=T))\
                          .then_inc(done[half], 16)

            def load_v(c, half):
                lb = index(c // CPB)
                need(sp, pv_done, PAIRS * (c - 1) + 4 * (half + 1))
                cs = slice(half * 512, (half + 1) * 512)
                sp.dma_start(v[:, cs], v_d[lb, :, cs]).then_inc(v_in[half], 16)

            def load_res(c, t, layer):
                need(sp, y_out[t], 16 * c)
                src = xT if layer == 0 else x1_d
                sp.dma_start(res[:, t, :], src[t * P:(t + 1) * P, bass.ds((c - layer * NCH + 1) * Q - Q, Q)]).then_inc(r_in[t], 16)

            for n in range(4, len(TILES)):
                w_load(n)
                l, w = TILES[n]
                if n == 12:
                    sp.wait_ge(c_lo_done, 4)
                    load_x(0, 0)
                if n == 8:
                    sp.wait_ge(consts, BIAS_STEPS)
                    for i, part in enumerate((m_hi, m_lo)):
                        for a in range(2):
                            sp.dma_start(sup_d[2 * a + i, :].rearrange("(r n) -> r n", n=P),
                                         part[a * MR // 2:(a + 1) * MR // 2, :].bitcast(F32)).then_inc(sup_out, 16)
                if l is not None and w in (W_TILES - 4, W_TILES - 2):
                    part, dst, split = (k_hi, kh_d, k_hi_done) if w == W_TILES - 4 else (k_lo, kl_d, k_lo_done)
                    sp.wait_ge(split, 4 * (l + 1))
                    for b in range(B):
                        sp.dma_start(dst[l * B + b, :, :].rearrange("p (m t) -> p m t", t=T),
                                     part.rearrange("p (m b t) -> p m b t", b=B, t=T)[:, :, b, :].bitcast(F32))\
                          .then_inc(k_out, 16)
                if l == 1 and w == 3:
                    sp.wait_ge(k_out, 16 * K_STORES)
                    sp.wait_ge(ext_out, 16 * LAYERS)
                    load_k(0, 0, 0)
                if l == 1 and w == 5:
                    sp.wait_ge(v_out, 16 * B)
                    load_v(0, 0)
                if l == 1 and w == 7:
                    sp.wait_ge(sup_out, 16 * 4)
                    sp.wait_ge(pool_c, POOL_CONSTS)
                    load_sup(0)
            load_k(0, 1, 0)
            load_v(0, 1)
            sp.wait_ge(k_out, 16 * K_STORES * LAYERS)
            sp.wait_ge(v_out, 16 * B * LAYERS)
            sp.wait_ge(w_lo_done, len(TILES))

            def spread(k, c, i):
                need(sp, on_done, k - 1)
                if i % 4 == 0:
                    n = 2 * c + i // 4
                    sp.wait_ge(rec_raw, n + 1)
                    for h in range(2):
                        sp.dma_start(rec_d[i // 4, h, :, :], rec[h:P:32, :]).then_inc(rec_out, 16)
                    sp.wait_ge(rec_out, 32 * (n + 1))
                sp.dma_start(bc[:, i % 2, :],
                             rec_d[i // 4, :, i % 4, :].unsqueeze(1).to_broadcast([2, D, Q])).then_inc(bc_in[i % 2], 16)

            def step(g, s, layer):
                if s % 4:
                    for off in (0, 1) if s % 4 == 1 else (1,):
                        norm = pair(g, s, off - NORM)
                        if norm:
                            spread(*norm)
                inside = not isinstance(g, int)
                nxt = inside or g + 1 < TOTAL
                here = inside or 0 <= g < TOTAL
                before = inside or g >= 1
                if isinstance(g, int):
                    if g == NCH - 1:
                        need(sp, sl_lo[0], s - 1)
                        sp.dma_start(w_st[:, s % 2, :, :], Wq[1, :, s * P:(s + 1) * P].rearrange("(k p) n -> p k n", p=P))\
                          .then_inc(sl_in[0][s % 2], 16)
                    if g in (0, NCH):
                        l = g // NCH
                        if l and s == 0:
                            sp.wait_ge(sl_lo[0], PAIRS)
                        need(sp, sl_lo[1], l * PAIRS + s - 1)
                        hf, t = s // 4, s % 4
                        src = Wo[l, hf * 4 * P:(hf + 1) * 4 * P, t * P:(t + 1) * P]
                        sp.dma_start(w_st[:, s % 2, :, :], src.rearrange("(k p) n -> p k n", p=P)).then_inc(sl_in[1][s % 2], 16)
                if here and nxt:
                    if s == 0:
                        load_x(g + 1, layer_of(g + 1, layer))
                    if s == 5:
                        load_sup(g + 1)
                    if s == 4:
                        load_k(g + 1, 0, layer_of(g + 1, layer))
                    if s == 5:
                        load_v(g + 1, 0)
                if here and before:
                    if s == 0:
                        load_k(g, 1, layer_of(g, layer))
                    if s == 1:
                        load_v(g, 1)
                if before and s == 0:
                    load_res(g - 1, XT - 1, layer_of(g - 1, layer))
                if here and s >= 5:
                    load_res(g, s - 5, layer_of(g, layer))
                if before and s >= 4:
                    t, c, lc = s - 4, g - 1, layer_of(g - 1, layer)
                    dst = yT if lc == LAYERS - 1 else x1_d
                    sp.wait_ge(res_done, PAIRS * c + s + 1)
                    sp.dma_start(dst[t * P:(t + 1) * P, bass.ds((c - lc * NCH + 1) * Q - Q, Q)], res[:, t, :]).then_inc(y_out[t], 16)

            chunks(sp, step)
            for t in range(XT):
                sp.wait_ge(y_out[t], 16 * TOTAL)

        @block.tensor
        def _(pe):
            def project_q(k, c, i, products):
                if products[0] == 0:
                    if i == 0:
                        pe.wait_ge(x_hi_done, XT * (c + 1))
                    if isinstance(c, int) and c == NCH:
                        pe.wait_ge(sl_lo[0], i + 1)
                    need(pe, qhi_done, 2 * k)
                    need(pe, qlo_done, 2 * k)
                for n in products:
                    wt, xx = ((wq_hi, x_hi), (wq_lo, x_hi), (wq_hi, x_lo))[n // XT]
                    t = n % XT
                    if i == 0 and n == 2 * XT:
                        pe.wait_ge(x_lo_done, XT * (c + 1))
                    mm = pe.matmul(q_ps[:, :], wt[:, i, t, :], xx[:, t, :], start=(n == 0), stop=(n == 3 * XT - 1))
                if products[-1] == 3 * XT - 1:
                    mm.then_inc(q_done, 1)

            for l in range(LAYERS):
                for w in range(W_TILES):
                    n, kk, sl = l * W_TILES + w, w % KTL, w % 4
                    if n == KV - 1:
                        pe.wait_ge(k_lo_done, 4 * LAYERS)
                        pe.wait_ge(w_lo_done, len(TILES) - 1)
                        project_q(0, 0, 0, range(3 * XT))
                    if not l and w < KTL and w % 2 == 0:
                        pe.wait_ge(c_lo_done, w // 2 + 1)
                    pe.wait_ge(w_lo_done, TILES.index((l, w)) + 1)
                    parts = ((s_hi[sl], c_hi), (s_lo[sl], c_hi), (s_hi[sl], c_lo))
                    if w < KTL:
                        if w == 0 and l:
                            pe.wait_ge(k_lo_done, 4 * l)
                        for m in range(PAIRS):
                            for i, (wt, cx) in enumerate(parts):
                                mm = pe.matmul(banks[m // 2][:, (m % 2) * BT:(m % 2 + 1) * BT],
                                               wt[:, m * P:(m + 1) * P], cx[:, kk, :],
                                               start=(kk == 0 and i == 0 and m % 2 == 0),
                                               stop=(kk == KTL - 1 and i == 2), skip_group_check=True)
                    else:
                        if w == KTL and l:
                            pe.wait_ge(v_done, 4 * l)
                        for b in range(B):
                            for nh in range(2):
                                for i, (wt, cx) in enumerate(parts):
                                    mm = pe.matmul(banks[4 + 2 * b + nh][:, :], cx[:, kk, b * T:(b + 1) * T],
                                                   wt[:, nh * 512:(nh + 1) * 512],
                                                   start=(kk == 0 and i == 0), stop=(kk == KTL - 1 and i == 2))
                    mm.then_inc(w_used, 1)
            pe.wait_ge(consts, DVE_CONSTS)
            pe.wait_ge(pool_c, POOL_CONSTS)

            def logits(k, c, i):
                if i % 4 == 0:
                    pe.wait_ge(kt_in[i // 4], 64 * (c + 1))
                pe.wait_ge(qdup_done, k + 1)
                pe.wait_ge(qlo_done, 2 * k + 2)
                pe.wait_ge(mrow_done, NB * (k + 1))
                need(pe, p_done, 2 * k)
                if isinstance(k, int) and k == 0:
                    pe.wait_ge(v_done, 4 * LAYERS)
                for h in range(2):
                    hd = 2 * i + h
                    pe.matmul(lg_ps[h][:, :], km[:, hd, :], qe[:, i % 2, h, :], start=True, stop=False)
                    pe.matmul(lg_ps[h][:, :], kt[:, hd, :], qt[:, i % 2, h, :], start=False, stop=True)\
                      .then_inc(lg_done, 1)

            def maxima(k, c, i, h):
                if i % 4 == 0 and h == 0:
                    pe.wait_ge(km_in[i // 4], 48 * (c + 1))
                if h == 0:
                    pe.wait_ge(mz_done, 2 * k + 2)
                pe.wait_ge(qhi_done, 2 * k + h + 1)
                for n in range(NB):
                    mm = pe.matmul(mx_ps[h][:, n * T:(n + 1) * T], qe[:, i % 2, h, n * P:(n + 1) * P],
                                   km[:, 2 * i + h, :], start=True, stop=True)
                mm.then_inc(mx_done, 1)

            def turn_maxima(k, c, i):
                pe.wait_ge(mred_done, 2 * k + 2)
                pe.transpose(mx_ps[0][:, 0:P], mneg[:, i % 2, :, :].rearrange("p n c -> p (n c)"), ident[:, :])\
                  .then_inc(mt_done, 1)

            def probs_v(k, c, i):
                if i % 4 == 0:
                    pe.wait_ge(v_in[i // 4], 16 * (c + 1))
                if isinstance(k, int) and k == PAIRS * TOTAL - 1:
                    pe.wait_ge(p_done, 2 * k + 2)
                need(pe, oun_done, k)
                for h in range(2):
                    hd = 2 * i + h
                    mm = pe.matmul(pv_ps[h * D:(h + 1) * D, :], v[:, hd * D:(hd + 1) * D], probs[:, i % 2, h, :],
                                   start=True, stop=True)
                mm.then_inc(pv_done, 1)

            def denominators(k, c, i):
                pe.wait_ge(fold_done, 2 * k + 2)
                need(pe, rec_raw, 2 * c + i // 4)
                for j in range(4):
                    mm = pe.matmul(sum_ps[32 * j:32 * j + 32, :], ssel[:, :], fold[:, j, :], start=True, stop=True)
                mm.then_inc(sum_done, 1)

            def project_out(k, c, i, lc):
                hf, t = i // 4, i % 4
                if lc or isinstance(c, int) and c == 0:
                    pe.wait_ge(sl_lo[1], lc * PAIRS + i + 1)
                need(pe, res_done, PAIRS * c if final(c) else k)
                for kk in range(4):
                    if t == 0:
                        pe.wait_ge(o_done, PAIRS * c + 4 * hf + kk + 1)
                    for n, (wt, oo) in enumerate(((wo_hi, o_hi), (wo_lo, o_hi), (wo_hi, o_lo))):
                        mm = pe.matmul(out_bank(c, i)[:, :], wt[:, hf, t, kk, :], oo[:, 4 * hf + kk, :],
                                       start=(kk == 0 and n == 0), stop=(kk == 3 and n == 2))
                mm.then_inc(out_done, 1)

            def last_units(c):
                for kk in range(4):
                    pe.wait_ge(o_done, PAIRS * c + 4 + kk + 1)
                    for t in range(4):
                        if kk == 0 and t == 1:
                            pe.wait_ge(res_done, PAIRS * c + 3)
                        for n, (wt, oo) in enumerate(((wo_hi, o_hi), (wo_lo, o_hi), (wo_hi, o_lo))):
                            mm = pe.matmul(out_bank(c, 4 + t)[:, :], wt[:, 1, t, kk, :], oo[:, 4 + kk, :],
                                           start=(kk == 0 and n == 0), stop=(kk == 3 and n == 2))
                        if kk == 3:
                            mm.then_inc(out_done, 1)

            def step(g, s, layer):
                now, ahead, far = pair(g, s, 0), pair(g, s, 1), pair(g, s, AHEAD)
                last, unit = pair(g, s, -1), pair(g, s, -PAIRS)
                if now:
                    logits(*now)
                if last:
                    probs_v(*last)
                    if last[2] % 4 == 3:
                        denominators(*last)
                if ahead:
                    maxima(*ahead, 0)
                if unit and ahead and not far:
                    maxima(*ahead, 1)
                    turn_maxima(*ahead)
                    ahead = None
                if ahead:
                    maxima(*ahead, 1)
                if unit and final(unit[1]) and s >= 4:
                    if s == 4:
                        last_units(unit[1])
                elif unit:
                    project_out(*unit, layer_of(unit[1], layer))
                if far and far[2] == 0 and isinstance(g, int) and g < 0:
                    pass
                elif far:
                    start = 0 if unit or not ahead else 6
                    if start:
                        project_q(*far, range(start))
                    if ahead:
                        turn_maxima(*ahead)
                    project_q(*far, range(start, 3 * XT))
                elif ahead:
                    turn_maxima(*ahead)

            chunks(pe, step)

        @block.scalar
        def _(act):
            act.wait_ge(pool_c, 3)
            nc.scalar.activation(warm[:, :], mneg[:, 0, 0, 0:1], ACT.Exp)
            act.dma_start(m_f, masks.rearrange("a (r n) -> (a r) n", n=P)).then_inc(small_in, 16)
            act.dma_start(ints[:, 0:2 * LAYERS * NI], idx.partition_broadcast(P)).then_inc(small_in, 16)
            act.dma_start(bo_s[:, :, :], bo.rearrange("p (l t) -> p l t", t=XT)).then_inc(small_in, 16)

            def q_hi(k, c, i):
                act.wait_ge(q_done, k + 1)
                for h in range(2):
                    need(act, lg_done, 2 * k + h - 3)
                    nc.scalar.copy(qe[0:D, i % 2, h, :], q_ps[h * D:(h + 1) * D, :]).then_inc(qhi_done, 1)

            def split_x(c):
                act.wait_ge(x_in, 16 * (c + 1))
                need(act, q_done, PAIRS * c)
                for t in range(XT):
                    nc.scalar.copy(x_hi[:, t, :], x_f[:, t, :]).then_inc(x_hi_done, 1)

            for n, (l, w) in enumerate(TILES):
                sl = n % 4
                if n < 4:
                    act.wait_ge(c_in[n], 16)
                    nc.scalar.copy(c_hi[:, 2 * n:2 * n + 2, :], c_f[:, 2 * n:2 * n + 2, :]).then_inc(c_hi_done, 1)
                act.wait_ge(w_in[sl], 16 * (n // 4 + 1))
                if l is not None:
                    need(act, w_used, l * W_TILES + w - 3)
                    nc.scalar.copy(s_hi[w % 4], stage[sl]).then_inc(w_hi_done, 1)
                else:
                    nc.scalar.copy(wq_hi[:, :, w, :], stage[sl].rearrange("p (m c) -> p m c", c=P)).then_inc(w_hi_done, 1)
                if l == 1 and w == 2:
                    split_x(0)
                if l is not None and w == KTL + 1:
                    act.wait_ge(w_used, l * W_TILES + KTL)
                    if l:
                        act.wait_ge(k_out, 16 * K_STORES * l)
                    for m in range(4):
                        nc.scalar.mul(k_hi[:, m * 512:(m + 1) * 512], banks[m][:, :], SCALE).then_inc(k_hi_done, 1)
                if n == len(TILES) - 1:
                    act.wait_ge(k_out, 16 * K_STORES * LAYERS)
                    q_hi(0, 0, 0)
                if (l, w) == (1, 1) or n == len(TILES) - 1:
                    lv = int(w != 1)
                    act.wait_ge(w_used, (lv + 1) * W_TILES)
                    if lv:
                        act.wait_ge(v_out, 16 * B * lv)
                    else:
                        act.wait_ge(consts, DVE_CONSTS)
                    for m in (2, 3):
                        nc.scalar.copy(v_s[m // 2][:, m % 2, :], banks[4 + m][:, :]).then_inc(v_done, 1)
                    act.wait_ge(v_done, 4 * (lv + 1))
                    for b in range(B):
                        act.dma_start(v_d[lv * B + b, :, :], v_s[b].rearrange("t n c -> t (n c)")).then_inc(v_out, 16)
            act.wait_ge(w_lo_done, len(TILES))

            def exps(k, c, i):
                need(act, pv_done, k - 1)
                need(act, fold_done, 2 * k - 2)
                for h in range(2):
                    act.wait_ge(lg_done, 2 * k + h + 1)
                    nc.scalar.activation(probs[:, i % 2, h, :], lg_ps[h][:, :], ACT.Exp).then_inc(p_done, 1)

            def halves(k, c, i):
                if i % 4 == 0:
                    need(act, sum_done, 2 * c + i // 4)
                if isinstance(k, int) and k == 2:
                    act.wait_ge(v_out, 16 * B * LAYERS)
                for h in range(2):
                    act.wait_ge(p_done, 2 * k + h + 1)
                    nc.scalar.copy(fold[h * D:(h + 1) * D, i % 4, :], probs[(1 - h) * D:(2 - h) * D, i % 2, h, :])\
                      .then_inc(half_done, 1)

            def q_dup(k, c, i):
                act.wait_ge(qhi_done, 2 * k + 2)
                nc.scalar.copy(qt[0:D, i % 2, :, :], qe[0:D, i % 2, :, :]).then_inc(qdup_done, 1)

            def copy_o(k, c, i):
                act.wait_ge(pv_done, k + 1)
                need(act, o_done, k - 3)
                nc.scalar.copy(o_f[:, i % 4, :], pv_ps[:, :]).then_inc(oun_done, 1)

            def max_rows(k, c, i):
                act.wait_ge(mt_done, k + 1)
                for n in range(NB):
                    nc.scalar.copy(qe[MRW:P, i % 2, :, n * P:(n + 1) * P],
                                   mx_ps[0][32 * n:32 * n + 32, 0:P].unsqueeze(1).to_broadcast([32, 2, P])).then_inc(mrow_done, 1)

            def step(g, s, layer):
                now, ahead, last = pair(g, s, 0), pair(g, s, 1), pair(g, s, -1)
                if ahead and not (isinstance(g, int) and g < 0):
                    q_hi(*ahead)
                if now:
                    exps(*now)
                if s == 6 and (not isinstance(g, int) or 0 <= g < TOTAL - 1):
                    split_x(g + 1)
                if now:
                    halves(*now)
                if ahead:
                    q_dup(*ahead)
                if ahead:
                    max_rows(*ahead)
                if last:
                    copy_o(*last)

            chunks(act, step)

        @block.vector
        def _(dve):
            chain = [0]

            def link(ins):
                chain[0] += 1
                ins.then_inc(consts, 1)
                dve.wait_ge(consts, chain[0])

            def bias_rows():
                rows = m_f
                link(nc.vector.tensor_scalar(rows, rows, -1.0, 1.0, ALU.mult, ALU.add))
                link(nc.vector.tensor_scalar(rows, rows, -SUPPRESS / 2, None, ALU.mult))
                link(nc.vector.tensor_copy(m_hi, rows))
                link(nc.vector.tensor_tensor(m_lo, rows, m_hi, ALU.subtract))

            def is_row(dst, lo, hi):
                row = row_s[:, 0:1]
                link(nc.vector.tensor_scalar(dst, row, float(lo), None, ALU.is_ge))
                link(nc.vector.scalar_tensor_tensor(out=dst, in0=row, scalar=float(hi), in1=dst,
                                                    op0=ALU.is_lt, op1=ALU.mult))

            def tables():
                dve.wait_ge(pool_c, 2)
                link(nc.vector.tensor_copy(tok[:, 0:T], ints[:, 64:64 + T]))
                link(nc.vector.tensor_copy(row_s[:, 0:1], ints[:, 32:33]))
                link(nc.vector.tensor_scalar(ident[:, :], tok[:, 0:P], row_s[:, 0:1], None, ALU.is_equal))

                for n, lo in enumerate((SUP, SUP + 2)):
                    is_row(row_s[:, 1 + n:2 + n], lo, lo + 2)
                for h in range(2):
                    is_row(row_s[:, 3 + h:4 + h], MRW + h, MRW + h + 1)

            def token_set(l, a, dst):
                at = (2 * l + a) * NI
                link(nc.vector.tensor_scalar(dst, tok[:, 0:T], idx_f[:, at:at + 1], None, ALU.is_equal))
                for n in range(at + 1, at + NI):
                    link(nc.vector.scalar_tensor_tensor(out=dst, in0=tok[:, 0:T], scalar=idx_f[:, n:n + 1],
                                                        in1=dst, op0=ALU.is_equal, op1=ALU.max))

            def indicators(l):
                link(nc.vector.tensor_scalar(ind_n, ind_b, -1.0, 1.0, ALU.mult, ALU.add))
                link(nc.vector.tensor_tensor(ind_a, ind_a, ind_n, ALU.mult))
                for h in range(2):
                    link(nc.vector.tensor_scalar(ind_n, ind_a, row_s[:, 1:2], row_s[:, 3 + h:4 + h], ALU.mult, ALU.add))
                    link(nc.vector.scalar_tensor_tensor(out=ext[:, l, h, :], in0=ind_b, scalar=row_s[:, 2:3], in1=ind_n,
                                                        op0=ALU.mult, op1=ALU.add))

            def split_x(c):
                for t in range(XT):
                    dve.wait_ge(x_hi_done, XT * c + t + 1)
                    nc.vector.tensor_tensor(x_lo[:, t, :], x_f[:, t, :], x_hi[:, t, :], ALU.subtract).then_inc(x_lo_done, 1)

            def q_lo(k, c, i):
                for h in range(2):
                    dve.wait_ge(qhi_done, 2 * k + h + 1)
                    need(dve, lg_done, 2 * k + h - 3)
                    nc.vector.tensor_tensor(qt[D:P, i % 2, h, :], q_ps[h * D:(h + 1) * D, :], qe[0:D, i % 2, h, :],
                                            ALU.subtract).then_inc(qlo_done, 1)

            tables()
            for n, (l, w) in enumerate(TILES):
                sl = n % 4
                if n < 4:
                    dve.wait_ge(c_hi_done, n + 1)
                    ks = slice(2 * n, 2 * n + 2)
                    nc.vector.tensor_tensor(c_lo[:, ks, :], c_f[:, ks, :], c_hi[:, ks, :], ALU.subtract).then_inc(c_lo_done, 1)
                dve.wait_ge(w_hi_done, n + 1)
                if l is not None:
                    nc.vector.tensor_tensor(s_lo[w % 4], stage[sl], s_hi[w % 4], ALU.subtract).then_inc(w_lo_done, 1)
                else:
                    nc.vector.tensor_tensor(wq_lo[:, :, w, :], stage[sl].rearrange("p (m c) -> p m c", c=P), wq_hi[:, :, w, :],
                                            ALU.subtract).then_inc(w_lo_done, 1)
                if n == 4:
                    dve.wait_ge(small_in, 16 * 3)
                    link(nc.vector.tensor_copy(idx_f, ints[:, 0:2 * LAYERS * NI]))
                    link(nc.vector.tensor_scalar(idx_w, idx_f, 0.0, float(T), ALU.is_lt, ALU.mult))
                    link(nc.vector.tensor_tensor(idx_f, idx_f, idx_w, ALU.add))
                    bias_rows()
                if l == 0 and w in (5, 7):
                    for a, dst in enumerate((ind_a, ind_b)):
                        token_set(w // 7, a, dst)
                if l == 0 and w in (6, 10):
                    indicators(w // 10)
                if n == len(TILES) - 1:
                    dve.wait_ge(k_out, 16 * K_STORES * LAYERS)
                    q_lo(0, 0, 0)
                if (l, w) == (1, 1) or n == len(TILES) - 1:
                    lv = int(w != 1)
                    dve.wait_ge(w_used, (lv + 1) * W_TILES)
                    if lv:
                        dve.wait_ge(v_out, 16 * B * lv)
                    for m in (0, 1):
                        nc.vector.tensor_copy(v_s[m // 2][:, m % 2, :], banks[4 + m][:, :]).then_inc(v_done, 1)
                if l == 1 and w == 2:
                    split_x(0)
                if l is not None and w == KTL + 1:
                    for m in range(4):
                        dve.wait_ge(k_hi_done, 4 * l + m + 1)
                        ms = slice(m * 512, (m + 1) * 512)
                        nc.vector.scalar_tensor_tensor(out=k_lo[:, ms], in0=banks[m][:, :], scalar=SCALE, in1=k_hi[:, ms],
                                                       op0=ALU.mult, op1=ALU.subtract).then_inc(k_lo_done, 1)
            assert chain[0] == DVE_CONSTS, chain[0]

            def row_max(k, c, i, h):
                dve.wait_ge(mx_done, 2 * k + h + 1)
                if h == 0:
                    need(dve, mt_done, k - 1)
                nc.vector.tensor_reduce(mneg[:, i % 2, :, h], mx_ps[h][:, :].rearrange("p (n t) -> p n t", t=T), AX_X,
                                        ALU.max, negate=True).then_inc(mred_done, 1)

            def normalise(k, c, i):
                dve.wait_ge(bc_in[i % 2], 16 * (PAIRS // 2 * c + i // 2 + 1))
                dve.wait_ge(oun_done, k + 1)
                nc.vector.tensor_tensor(o_f[:, i % 4, :], o_f[:, i % 4, :], bc[:, i % 2, :], ALU.mult).then_inc(on_done, 1)

            def split_o(k, c, i):
                need(dve, out_done, PAIRS * c + 4 * (i // 4) - 4)
                dve.wait_ge(on_done, k + 1)
                nc.vector.tensor_copy(o_hi[:, i, :], o_f[:, i % 4, :]).then_inc(oh_done, 1)
                dve.wait_ge(oh_done, k + 1)
                nc.vector.tensor_tensor(o_lo[:, i, :], o_f[:, i % 4, :], o_hi[:, i, :], ALU.subtract).then_inc(o_done, 1)

            def reciprocals(k, c, i):
                n = 2 * c + i // 4
                dve.wait_ge(sum_done, n + 1)
                nc.vector.reciprocal(rec[:, :], sum_ps[:, :]).then_inc(rec_raw, 1)

            def add_out(k, c, i, lc):
                hf, t = i // 4, i % 4
                bank = out_bank(c, i)
                dve.wait_ge(out_done, k + 1)
                if hf == 0:
                    dve.wait_ge(r_in[t], 16 * (c + 1))
                    ins = nc.vector.scalar_tensor_tensor(out=res[:, t, :], in0=bank[:, :], scalar=bo_s[:, lc, t:t + 1],
                                                         in1=res[:, t, :], op0=ALU.add, op1=ALU.add)
                else:
                    dve.wait_ge(res_done, k - 3)
                    ins = nc.vector.tensor_tensor(res[:, t, :], bank[:, :], res[:, t, :], ALU.add)
                ins.then_inc(res_done, 1)

            def split_slice(which, n, hi, lo, used_by, used):
                dve.wait_ge(sl_in[which][n % 2], 16 * (n // 2 + 1))
                dve.wait_ge(used_by, used)
                nc.vector.tensor_copy(hi, w_st[:, n % 2, :, :]).then_inc(sl_hi[which], 1)
                dve.wait_ge(sl_hi[which], n + 1)
                nc.vector.tensor_tensor(lo, w_st[:, n % 2, :, :], hi, ALU.subtract).then_inc(sl_lo[which], 1)

            def step(g, s, layer):
                ahead, last, norm, unit = pair(g, s, 1), pair(g, s, -1), pair(g, s, -NORM), pair(g, s, -PAIRS)
                if norm and s % 4 == 0:
                    normalise(*norm)
                if ahead and not (isinstance(g, int) and g < 0):
                    q_lo(*ahead)
                if norm and s % 4 == 0:
                    split_o(*norm)
                if ahead:
                    row_max(*ahead, 0)
                    row_max(*ahead, 1)
                if s == 6 and (not isinstance(g, int) or 0 <= g < TOTAL - 1):
                    split_x(g + 1)
                if s == 1 and unit and final(unit[1]):
                    for i in range(3):
                        add_out(PAIRS * unit[1] + i, unit[1], i, LAYERS - 1)
                if norm and s % 4:
                    normalise(*norm)
                    split_o(*norm)
                if last and last[2] % 4 == 3:
                    reciprocals(*last)
                if unit and final(unit[1]):
                    for i in (3, 4) if s == 4 else [s] if s > 4 else []:
                        add_out(PAIRS * unit[1] + i, unit[1], i, LAYERS - 1)
                elif unit:
                    add_out(*unit, layer_of(unit[1], layer))
                if isinstance(g, int) and g == NCH - 1:
                    split_slice(0, s, wq_hi[:, s, :, :], wq_lo[:, s, :, :], q_done, PAIRS * g + s + 1)
                wo_parts = [w[:, s // 4, s % 4, :, :] for w in (wo_hi, wo_lo)]
                if isinstance(g, int) and g == 0:
                    split_slice(1, s, *wo_parts, w_used, KV)
                if isinstance(g, int) and g == NCH:
                    split_slice(1, PAIRS + s, *wo_parts, out_done, PAIRS * (g - 1) + s + 1)

            chunks(dve, step)

        @block.gpsimd
        def _(pool):
            nc.gpsimd.iota(ints[:, 64:64 + T], pattern=[[1, T]], base=0, channel_multiplier=0).then_inc(pool_c, 1)
            nc.gpsimd.iota(ints[:, 32:33], pattern=[[0, 1]], base=0, channel_multiplier=1).then_inc(pool_c, 1)
            nc.gpsimd.memset(mneg[:, :, :, :], 0.0).then_inc(pool_c, 1)
            nc.gpsimd.memset(ssel[:, :], 1.0).then_inc(pool_c, 1)
            pool.wait_ge(pool_c, 4)
            nc.gpsimd.memset(ssel[D:P, 0:1], 0.0).then_inc(pool_c, 1)
            pool.wait_ge(pool_c, 5)
            nc.gpsimd.memset(ssel[0:D, 1:2], 0.0).then_inc(pool_c, 1)
            pool.wait_ge(consts, DVE_CONSTS)
            for l in range(LAYERS):
                pool.dma_start(ext_d[l, :, :], ext[SUP:P, l, :, :].bitcast(F32).rearrange("p a t -> p (a t)")).then_inc(ext_out, 16)
            pool.wait_ge(ext_out, 16 * LAYERS)
            pool.wait_ge(pool_c, POOL_CONSTS - 1)
            nc.gpsimd.memset(sup_c[SUP:P, :].bitcast(F32), 0.0).then_inc(pool_c, 1)
            pool.wait_ge(pool_c, POOL_CONSTS)
            pool.wait_ge(k_out, 16 * K_STORES * LAYERS)

            def rows(k, c, i):
                need(pool, lg_done, 2 * k - 2)
                need(pool, fold_done, 2 * k - 4)
                if i == 0:
                    pool.wait_ge(sup_in, 16 * (c + 1))
                for h in range(2):
                    src = sup_c[SUP:P, :].bitcast(F32)
                    nc.gpsimd.tensor_tensor(qe[SUP:P, i % 2, h, :], src, src, ALU.add).then_inc(mz_done, 1)

            def folds(k, c, i):
                pool.wait_ge(mz_done, min(2 * k + 6, 2 * PAIRS * TOTAL) if isinstance(k, int) else 2 * k + 6)
                for h in range(2):
                    at = slice(h * D, (h + 1) * D)
                    pool.wait_ge(half_done, 2 * k + h + 1)
                    if h:
                        pool.wait_ge(fold_done, 2 * k + 1)
                    nc.gpsimd.tensor_tensor(fold[at, i % 4, :], fold[at, i % 4, :], probs[at, i % 2, h, :],
                                            ALU.add).then_inc(fold_done, 1)

            def step(g, s, layer):
                now, far = pair(g, s, 0), pair(g, s, AHEAD)
                if far:
                    rows(*far)
                if now:
                    folds(*now)

            chunks(pool, step)


def kernel(**inputs):
    import numpy as np
    import concourse.bacc as bacc
    from concourse.bass_utils import run_bass_kernel_spmd

    a = {k: np.asarray(x) for k, x in inputs.items()}
    Bn, HWn, Cn = a["x"].shape
    lay = ("L0_xattn_", "L1_xattn_")
    arrays = {
        "xT": np.ascontiguousarray(a["x"].reshape(Bn * HWn, Cn).T),
        "ctxT": np.ascontiguousarray(a["ctx_2048"].reshape(-1, a["ctx_2048"].shape[-1]).T),
        "masks": np.stack([a["mask_S_fk1"], a["mask_S_fk0"]]),
        "Wk": np.stack([a[l + "Wk"] for l in lay]),
        "Wv": np.stack([a[l + "Wv"] for l in lay]),
        "Wq": np.stack([a[l + "Wq"] for l in lay]),
        "Wo": np.stack([a[l + "Wo"] for l in lay]),
        "bo": np.ascontiguousarray(np.stack([a[l + "bo"] for l in lay]).reshape(-1, P).T),
        "idx": np.concatenate([a[l + "token_indices_" + s] for l in lay for s in "AB"])[None, :],
    }
    nc = bacc.Bacc("TRN2", target_bir_lowering=False, num_devices=1)
    args = [nc.dram_tensor(n, x.shape, mybir.dt.from_np(x.dtype), kind="ExternalInput").ap() for n, x in arrays.items()]
    yT = nc.dram_tensor("yT", (Cn, Bn * HWn), F32, kind="ExternalOutput").ap()
    two_cross_attentions(nc, *args, yT)
    r = run_bass_kernel_spmd(nc, [arrays], core_ids=[0])
    return np.ascontiguousarray(r.results[0]["yT"].T).reshape(Bn, HWn, Cn)
```
